# Optimizing a Trainium2 kernel written in Bass

```python
import numpy as np
import jax
import jax.numpy as jnp

def _softmax(x, axis=-1):
    return jax.nn.softmax(x, axis=axis)

def _gelu(x):
    return jax.nn.gelu(x, approximate=True)

def _silu(x):
    return jax.nn.silu(x)

def _sigmoid(x):
    return jax.nn.sigmoid(x)

def _layernorm(x, axis=-1, eps=1e-05):
    m = jnp.mean(x, axis=axis, keepdims=True)
    v = jnp.var(x, axis=axis, keepdims=True)
    return (x - m) / jnp.sqrt(v + eps)

def _scatter_add(tgt, idx, src, axis=0):
    return tgt.at[idx].add(src)

def _segment_sum(src, seg, n):
    return jax.ops.segment_sum(src, seg, n)
kernel_name = 'mk_gnn_preln_d2_gnn_r8_6b447d'

def setup_inputs(seed: int=0):
    np.random.seed(seed)
    _w = jnp.asarray

    def _rec_inputs():
        import jax
        import jax.numpy as jnp
        _gk = jax.random.key(seed)
        x = -6.415e-05 + 1 * jax.random.normal(jax.random.fold_in(_gk, 1), (1250, 512), jnp.float32)
        src = jax.random.randint(jax.random.fold_in(_gk, 2), (40000,), 0, 1250, jnp.int32)
        dst = jnp.minimum((1250 * jax.random.uniform(jax.random.fold_in(_gk, 3), (40000,)) ** 2.0).astype(jnp.int32), 9999)
        _o = jnp.argsort(dst, stable=True)
        src = src[_o]
        dst = dst[_o]
        edge_type_32 = jax.random.randint(jax.random.fold_in(_gk, 13), (40000,), 0, 32, jnp.int32)
        edge_weight1 = jax.random.uniform(jax.random.fold_in(_gk, 14), (40000, 1), jnp.float32, 0.0, 0.999996)
        return (x, src, dst, edge_type_32, edge_weight1)
    x, src, dst, edge_type_32, edge_weight1 = _rec_inputs()

    def _L0_gnn_setup():
        import jax, jax.numpy as jnp
        import numpy as np
        N_NODES = 2500
        N_EDGES = 40000
        IN_FEAT = 512
        OUT_FEAT = 512
        NUM_RELS = 32
        NUM_BASES = 8
        key = jax.random.key(seed)
        ks = jax.random.split(key, 8)
        x = jax.random.normal(ks[0], (N_NODES, IN_FEAT), dtype=jnp.float32)
        bases = jax.random.normal(ks[1], (NUM_BASES, IN_FEAT, OUT_FEAT), dtype=jnp.float32) * (1.0 / np.sqrt(IN_FEAT))
        w_comp = jax.random.normal(ks[2], (NUM_RELS, NUM_BASES), dtype=jnp.float32) * (1.0 / np.sqrt(NUM_BASES))
        h_bias = jnp.zeros((OUT_FEAT,), dtype=jnp.float32)
        norm = jax.random.uniform(ks[3], (N_EDGES, 1), dtype=jnp.float32)
        src = jax.random.randint(ks[4], (N_EDGES,), 0, N_NODES, dtype=jnp.int32)
        dst = jax.random.randint(ks[5], (N_EDGES,), 0, N_NODES, dtype=jnp.int32)
        etype = jnp.sort(jax.random.randint(ks[6], (N_EDGES,), 0, NUM_RELS, dtype=jnp.int32))
        return {'x': x, 'bases': bases, 'w_comp': w_comp, 'h_bias': h_bias, 'norm': norm, 'src': src, 'dst': dst, 'etype': etype}
    _L0_gnn_all = _L0_gnn_setup()
    _L0_gnn_in = {k: v for k, v in _L0_gnn_all.items() if k in ('bases', 'w_comp', 'h_bias')}
    del _L0_gnn_all

    def _L1_gnn_setup():
        import jax, jax.numpy as jnp
        import numpy as np
        N_NODES = 6250
        N_EDGES = 50000
        IN_DIM = 512
        OUT_DIM = 512
        key = jax.random.key(seed)
        k1, k2, k3, k4 = jax.random.split(key, 4)
        x = jax.random.normal(k1, (N_NODES, IN_DIM), dtype=jnp.float32)
        edge_index = jax.random.randint(k2, (2, N_EDGES), 0, N_NODES, dtype=jnp.int64)
        W = jax.random.normal(k3, (OUT_DIM, IN_DIM), dtype=jnp.float32) / np.sqrt(IN_DIM)
        b = jax.random.normal(k4, (OUT_DIM,), dtype=jnp.float32) * 0.01
        return {'x': x, 'edge_index': edge_index, 'W': W, 'b': b}
    _L1_gnn_all = _L1_gnn_setup()
    _L1_gnn_in = {k: v for k, v in _L1_gnn_all.items() if k in ('W', 'b')}
    del _L1_gnn_all
    return {'x': x, 'src': src, 'dst': dst, 'edge_type_32': edge_type_32, 'edge_weight1': edge_weight1, 'L0_gnn_bases': _L0_gnn_in['bases'], 'L0_gnn_w_comp': _L0_gnn_in['w_comp'], 'L0_gnn_h_bias': _L0_gnn_in['h_bias'], 'L1_gnn_W': _L1_gnn_in['W'], 'L1_gnn_b': _L1_gnn_in['b']}

def reference(x, src, dst, edge_type_32, edge_weight1, L0_gnn_bases, L0_gnn_w_comp, L0_gnn_h_bias, L1_gnn_W, L1_gnn_b):
    import jax
    import jax.numpy as jnp

    def _L0_gnn_ref(x, bases, w_comp, h_bias, norm, src, dst, etype):
        import jax, jax.numpy as jnp
        import numpy as np
        N_NODES = 2500
        N_EDGES = 40000
        IN_FEAT = 512
        OUT_FEAT = 512
        NUM_RELS = 32
        NUM_BASES = 8
        n_nodes = x.shape[0]
        weight = jnp.einsum('rb,bio->rio', w_comp, bases)
        h_rel = jnp.einsum('ni,rio->rno', x, weight)
        msg = h_rel[etype, src] * norm
        out = jax.ops.segment_sum(msg, dst, num_segments=n_nodes)
        out = out + h_bias
        return out

    def _L1_gnn_ref(x, edge_index, W, b):
        import jax, jax.numpy as jnp
        import numpy as np
        N_NODES = 6250
        N_EDGES = 50000
        IN_DIM = 512
        OUT_DIM = 512
        n = x.shape[0]
        loops = jnp.arange(n, dtype=edge_index.dtype)
        row = jnp.concatenate([edge_index[0], loops])
        col = jnp.concatenate([edge_index[1], loops])
        deg = jax.ops.segment_sum(jnp.ones(row.shape[0], dtype=x.dtype), row, num_segments=n)
        dis = jax.lax.rsqrt(deg)
        norm = dis[row] * dis[col]
        h = x @ W.T + b
        out = jax.ops.segment_sum(norm[:, None] * h[row], col, num_segments=n)
        return jax.nn.relu(out)
    edge_index = jnp.stack([src, dst])
    h = jnp.maximum(_layernorm(x, axis=-1), 0.0)
    x = x + _L0_gnn_ref(h, L0_gnn_bases, L0_gnn_w_comp, L0_gnn_h_bias, edge_weight1, src, dst, edge_type_32)
    h = jnp.maximum(_layernorm(x, axis=-1), 0.0)
    x = x + _L1_gnn_ref(h, edge_index, L1_gnn_W, L1_gnn_b)
    return x

_drawn_inputs = setup_inputs


def setup_inputs(seed=0):
    import zlib

    import numpy as np

    out = dict(_drawn_inputs(seed))
    spreads = {'L0_gnn_h_bias': (0.0, 0.269)}
    factors = {'L1_gnn_b': 8.0}
    for name, (base, spread) in spreads.items():
        noise = np.random.default_rng([zlib.crc32(name.encode()), seed]).standard_normal(out[name].shape)
        drawn = base * np.exp(spread * noise) if base else spread * noise
        out[name] = jnp.asarray(drawn.astype(out[name].dtype))
    for name, factor in factors.items():
        out[name] = (out[name] * factor).astype(out[name].dtype)
    return out
```

```python
import concourse.bass as bass
from concourse import mybir
from contextlib import ExitStack


def gnn_kernel(nc, x, src, dst, etype, ew, bases, w_comp, h_bias, W1, b1, out):
    f32, bf16 = mybir.dt.float32, mybir.dt.bfloat16
    i32, u32 = mybir.dt.int32, mybir.dt.uint32
    ALU = mybir.AluOpType
    ACT = mybir.ActivationFunctionType
    AX = mybir.AxisListType
    P = 128

    N, D = x.shape
    E = src.shape[0]
    R, NB = w_comp.shape
    FT = D // P
    NT = -(-N // P)
    ROWS = [min(P, N - P * i) for i in range(NT)]
    GD = P // NB
    NG = -(-N // GD)
    TG = P // GD
    NGP = NT * TG
    UN = 8
    T0 = -(-((E - NG) // P + NG) // UN) * UN
    T1 = -(-((E - NT) // P + NT) // UN) * UN
    C0, C1 = -(-T0 // P), -(-T1 // P)
    T0P = T0 + UN
    T1P = T1 + UN
    EP, EC = 125, E // 125
    assert EP * EC == E
    PAD_DST = float(1 << 20)
    EPS = 1e-5
    SA, SB, SJ = -(-N // 32), 32, 2
    LEAD = 3
    NPB = 4

    rec_d = nc.dram_tensor("edge_records", [E + P, 4], f32, kind="Internal").ap()
    tab0_d = nc.dram_tensor("rows_layer0", [N, D], f32, kind="Internal").ap()
    tab1_d = nc.dram_tensor("rows_layer1", [N, D], f32, kind="Internal").ap()
    deg_d = nc.dram_tensor("degrees", [NT * P, 1], f32, kind="Internal").ap()
    wt_d = nc.dram_tensor("w1_transposed", [P, FT * D], f32, kind="Internal").ap()

    ctx = ExitStack()
    with ctx:
        def sb(name, shape, dt):
            return ctx.enter_context(nc.sbuf_tensor(name, shape, dt))

        def sem(name):
            return ctx.enter_context(nc.semaphore(name))

        Z = sb("Z", [P, NG, D], f32)
        gath = sb("gath", [P, UN, D], f32)
        base_ring = gath[:, :, :].rearrange("p (r f) o -> p r f o", r=2)
        sel = sb("sel", [P, 4, P], f32)
        val = sb("val", [P, T0P * NB], f32)
        val_v = val[:, :].rearrange("p (t b) -> p t b", b=NB)
        w1t = val[:, 0:FT * D].rearrange("p (f o) -> p f o", f=FT)
        dloc0 = sb("dloc0", [P, T0P], f32)
        src0 = sb("src0", [P, T0P], u32)
        dloc1 = sb("dloc1", [P, T1P], f32)
        src1 = sb("src1", [P, T1P], u32)
        slots = sb("slots", [1, T0P + T1P], i32)
        stage = sb("stage", [P, 2, UN // 2], u32)
        biases = sb("biases", [1, 2 * D], f32)
        ident = sb("ident", [P, P], f32)
        iota_f = sb("iota_f", [P, P], f32)
        ones = sb("ones", [P, P], f32)
        part_f = sb("part_f", [P, 1], f32)
        part_i = sb("part_i", [P, 1], i32)
        dis = sb("dis", [P, NT], f32)
        stats = sb("stats", [P, 6], f32)
        mv = sb("mv", [P, NT, 2], f32)
        rstd = sb("rstd", [P, NT], f32)
        nmr = sb("nmr", [P, NT], f32)
        eps_t = sb("eps_t", [P, 1], f32)
        flag = sb("flag", [1, 1], i32)

        flat = Z[:, :, :].rearrange("p g d -> p (g d)")
        early_at, late_at = [0], [64 * D]

        def words(dt, n):
            return n if dt in (f32, i32, u32) else -(-n // 2)

        def early(dt, n):
            a = early_at[0]
            early_at[0] += words(dt, n)
            assert early_at[0] <= 64 * D
            return flat[:, a:early_at[0]].bitcast(dt)

        def late(dt, n):
            a = late_at[0]
            late_at[0] += words(dt, n)
            assert late_at[0] <= NG * D
            return flat[:, a:late_at[0]].bitcast(dt)

        x_sb = early(f32, NT * D).rearrange("p (t d) -> p t d", t=NT)
        w_sb = early(f32, FT * D).rearrange("p (c i) -> p c i", c=FT)
        wt_sb = early(f32, FT * D).rearrange("p (f o) -> p f o", f=FT)
        iota_i = early(i32, P)
        e_src, e_dst, e_typ, e_nxt = (early(i32, EC)[0:EP, :] for _ in range(4))
        e_wt = early(f32, EC)[0:EP, :]
        rec = early(f32, EC * 4)[0:EP, :].rearrange("p (c k) -> p c k", k=4)
        past = early(f32, 4)
        viol = early(f32, EC)[0:EP, :]
        viol_s = early(f32, 1)[0:EP, :]
        t_i = early(i32, EC)[0:EP, :]
        ga, gb, sa, sbb = (early(bf16, EC)[0:EP, :] for _ in range(4))
        flat_ga, flat_gb, flat_sa, flat_sb = (early(bf16, n * EC)[0:EP, :] for n in (NT, TG, SA, SB))
        oh_ga, oh_gb, oh_sa, oh_sb = (a.rearrange("p (a c) -> p a c", c=EC) for a in (flat_ga, flat_gb, flat_sa, flat_sb))
        pm_i = early(i32, 4)
        pm_f = early(f32, 4)
        m_j, m_a, m_sj, m_sa = (early(f32, n) for n in (TG, NT, SJ, SA))
        tmp_g = early(f32, TG * TG).rearrange("p (b j) -> p b j", b=TG)
        prt_g = early(f32, TG)
        exp_g = early(f32, NGP)
        tmp_s = early(f32, SB * SJ).rearrange("p (b j) -> p b j", b=SB)
        prt_s = early(f32, SB)
        deg_ab = early(f32, SB)
        cnt, cum, nch, kend, dD, le, junk = (early(f32, NGP) for _ in range(7))
        nch_i = early(i32, NGP)
        cnt1, nch1, kend1, dD1 = (early(f32, NT) for _ in range(4))
        nch1_i = early(i32, NT)
        tt = early(f32, 1)
        gt = early(f32, C0 + C1)
        oacc = early(f32, C0 + C1)
        tri = early(f32, P)
        so_rec = early(f32, 4)[0:EP, :]
        so_dst = early(i32, 1)[0:EP, :]
        so_grp = early(f32, 1)[0:EP, :]
        so_oh = early(f32, NGP)[0:EP, :]
        so_prod = early(f32, NGP)[0:EP, :]
        so_posf = early(f32, 1)[0:EP, :]
        so_pos = early(u32, 1)[0:EP, :]
        so_next = early(f32, NGP)
        EARLY_END = early_at[0]

        offs = late(u32, C0 + C1)
        gsc = late(f32, C0 + C1)
        padr = late(f32, (C0 + C1) * P * 4).rearrange("p (c e k) -> p c e k", c=C0 + C1, k=4)
        typ16 = late(bf16, C0 * P).rearrange("p (c e) -> p c e", c=C0)
        wtT = late(f32, C0 * P)
        expand = late(bf16, P * R).rearrange("p (t r) -> p t r", r=R)
        oh_t = late(bf16, 2 * 4 * P).rearrange("p (s c) -> p s c", s=2)
        blk_i = late(i32, 1)
        blk, rel = late(f32, 1), late(f32, 1)
        wc = late(f32, NB)
        wbm = late(f32, 4)
        wblk = late(f32, 4 * NB).rearrange("p (t b) -> p t b", t=4)
        wparts = late(bf16, 3 * 4 * NB).rearrange("p (s n) -> p s n", s=3)

        PS = ctx.enter_context(nc.psum_tensor("PS", [P, 8, D], f32))
        iota_ps = PS[:, 7, 0:GD]

        s_iota = sem("s_iota")
        s_fill = sem("s_fill")
        s_edges = sem("s_edges")
        s_xin = sem("s_xin")
        s_win = sem("s_win")
        s_wc = sem("s_wc")
        s_bias = sem("s_bias")
        s_link = sem("s_link")
        s_rec = sem("s_rec")
        s_rec_out = sem("s_rec_out")
        s_ident = sem("s_ident")
        s_ohg = sem("s_ohg")
        s_cnt_part = sem("s_cnt_part")
        s_exp = sem("s_exp")
        s_cnt = sem("s_cnt")
        s_flag = sem("s_flag")
        s_ohs = sem("s_ohs")
        s_src_part = sem("s_src_part")
        s_src_masked = sem("s_src_masked")
        s_src_sum = sem("s_src_sum")
        s_deg_ab = sem("s_deg_ab")
        s_deg_out = sem("s_deg_out")
        s_deg_in = sem("s_deg_in")
        s_deg_sqrt = sem("s_deg_sqrt")
        s_dis = sem("s_dis")
        s_offs = sem("s_offs")
        s_slot_ps = sem("s_slot_ps")
        s_slots = sem("s_slots")
        s_padr = sem("s_padr")
        s_ploc = sem("s_ploc")
        s_ptr = sem("s_ptr")
        s_pev = sem("s_pev")
        s_expand = sem("s_expand")
        s_tb = sem("s_tb")
        s_oht = sem("s_oht")
        s_look = sem("s_look")
        s_val = sem("s_val")
        s_wparts = sem("s_wparts")
        s_stat0 = sem("s_stat0")
        s_sd0 = sem("s_sd0")
        s_nmr0 = sem("s_nmr0")
        s_h0 = sem("s_h0")
        s_tab0 = sem("s_tab0")
        s_wtr = sem("s_wtr")
        s_wev = sem("s_wev")
        s_wt_out = sem("s_wt_out")
        s_zero_src = sem("s_zero_src")
        s_zero_dma = sem("s_zero_dma")
        s_zero_pool = sem("s_zero_pool")
        s_so_v = sem("s_so_v")
        s_so_oh = sem("s_so_oh")
        s_so_mm = sem("s_so_mm")
        s_so_pos = sem("s_so_pos")
        s_so_out = sem("s_so_out")
        staged = [sem("s_staged0"), sem("s_staged1")]
        gathered = [[sem(f"s_gathered{n}_{k}") for k in range(UN)] for n in range(2)]
        selected = [sem("s_selected0"), sem("s_selected1")]
        mm_done = [sem("s_mm_done0"), sem("s_mm_done1")]
        added = [sem("s_added0"), sem("s_added1")]
        s_base = [sem("s_base0"), sem("s_base1")]
        s_base_used = sem("s_base_used")
        s_w1t = sem("s_w1t")
        s_zt = sem("s_zt")
        s_zte = [sem("s_zt_even"), sem("s_zt_odd")]
        s_accfree = [sem("s_accfree_even"), sem("s_accfree_odd")]
        s_xtr = sem("s_xtr")
        s_xre = [sem(f"s_xre{i}") for i in range(NT)]
        s_x1 = sem("s_x1")
        s_bn = sem("s_bn")
        s_stat1 = sem("s_stat1")
        s_sd1 = sem("s_sd1")
        s_rcp1 = sem("s_rcp1")
        s_nmr1 = sem("s_nmr1")
        s_h1 = sem("s_h1")
        s_htr = sem("s_htr")
        s_hev = sem("s_hev")
        s_u = sem("s_u")
        s_uev = sem("s_uev")
        s_tab1 = sem("s_tab1")
        s_relu = sem("s_relu")
        s_res = sem("s_res")
        s_out = sem("s_out")

        PASSES = [list(range(i, min(i + 4, NT))) for i in range(0, NT, 4)]
        GROUPS = [list(range(TG * i, min(TG * (i + 1), NG))) for i in range(NT)]
        VG = T0P // 16
        assert VG * 16 == T0P
        HALF = UN // 2
        ZDMA = EARLY_END // 2 // D * D
        POOL_END = 64 * D
        SLOT_X1, SLOT_U, SLOT_H, SLOT_HT, SLOT_X, SLOT_XT = range(6)

        def nslot(i, k):
            return Z[:, TG * i + k, :]

        def later_groups(p, b):
            if p + 1 == len(PASSES):
                return []
            gs = [g for i in PASSES[p + 1] for g in GROUPS[i]]
            per = -(-len(gs) // NB)
            return gs[per * b:per * (b + 1)]

        def prev_tile(p, k):
            return PASSES[p - 1][k] if p and 0 <= k < len(PASSES[p - 1]) else None

        def kept(p, c):
            tiles, ops = PASSES[p], []
            if all(r == P for r in (ROWS[i] for i in tiles)):
                there = Z[:, TG * tiles[0]:TG * (tiles[-1] + 1), :].rearrange("p (t s) d -> p t (s d)", s=TG)
                at = D * SLOT_XT + P * c
                return [(there[:, :, at:at + P], PS[:, c, 0:P * len(tiles)].rearrange("p (t n) -> p t n", n=P))]
            for k, i in enumerate(tiles):
                ops.append((nslot(i, SLOT_XT)[:, P * c:P * c + ROWS[i]], PS[:, c, P * k:P * k + ROWS[i]]))
            return ops

        block = ctx.enter_context(nc.Block())

        @block.sync
        def _(sp):
            sp.dma_start(e_dst, dst.rearrange("(p c) -> p c", p=EP)).then_inc(s_edges, 16)
            sp.wait_ge(s_fill, 1)
            sp.dma_start(e_nxt[0:EP - 1, :], dst[1:1 + (EP - 1) * EC].rearrange("(p c) -> p c", c=EC)).then_inc(s_edges, 16)
            sp.dma_start(e_nxt[EP - 1:EP, 0:EC - 1], dst[1 + (EP - 1) * EC:E].rearrange("(p c) -> p c", p=1)).then_inc(s_edges, 16)
            sp.dma_start(e_src, src.rearrange("(p c) -> p c", p=EP)).then_inc(s_edges, 16)
            sp.dma_start(e_typ, etype.rearrange("(p c) -> p c", p=EP)).then_inc(s_edges, 16)
            sp.dma_start(e_wt, ew.rearrange("(p c) k -> p (c k)", p=EP)).then_inc(s_edges, 16)
            full = N // P
            sp.dma_start(x_sb[:, 0:full, :], x[0:full * P, :].rearrange("(t p) d -> p t d", p=P)).then_inc(s_xin, 16)
            sp.dma_start(x_sb[0:ROWS[-1], full, :], x[full * P:N, :]).then_inc(s_xin, 16)
            for t in range(4):
                sp.dma_start(wc[R * t:R * (t + 1), :], w_comp[:, :]).then_inc(s_wc, 16)
            sp.dma_start(w_sb, W1.rearrange("(c p) i -> p c i", p=P)).then_inc(s_win, 16)
            sp.dma_start(biases[0:1, 0:D], h_bias.rearrange("(p d) -> p d", p=1)).then_inc(s_bias, 16)
            sp.dma_start(biases[0:1, D:2 * D], b1.rearrange("(p d) -> p d", p=1)).then_inc(s_bias, 16)
            sp.wait_ge(s_rec, 5)
            sp.dma_start(rec_d[0:E, :].rearrange("(p c) k -> p (c k)", p=EP),
                         rec.rearrange("p c k -> p (c k)")).then_inc(s_rec_out, 16)
            sp.dma_start(rec_d[E:E + P, :], past).then_inc(s_rec_out, 16)
            sp.wait_ge(s_h0, NT)
            sp.dma_start(tab0_d[0:full * P, :].rearrange("(t p) d -> p t d", p=P), x_sb[:, 0:full, :]).then_inc(s_tab0, 16)
            sp.dma_start(tab0_d[full * P:N, :], x_sb[0:ROWS[-1], full, :]).then_inc(s_tab0, 16)
            sp.wait_ge(s_wev, FT)
            sp.dma_start(wt_d[:, :], wt_sb.rearrange("p f o -> p (f o)")).then_inc(s_wt_out, 16)
            sp.wait_ge(s_deg_ab, 1)
            sp.dma_start(deg_d[:, :].rearrange("(a b) k -> a (b k)", b=SB), deg_ab[0:SA, :]).then_inc(s_deg_out, 16)
            sp.wait_ge(s_deg_out, 16)
            sp.dma_start(dis[:, :], deg_d[:, :].rearrange("(t p) k -> p (t k)", p=P),
                         allow_slow_non_contiguous=True).then_inc(s_deg_in, 16)
            sp.wait_ge(s_tab0, 32)
            sp.wait_ge(s_wt_out, 16)
            sp.wait_ge(s_zero_src, 1)
            sp.dma_start(flat[:, 0:ZDMA].rearrange("p (n d) -> p n d", d=D),
                         sel[:, :, :].rearrange("p s c -> p (s c)").unsqueeze(1).to_broadcast([P, ZDMA // D, D])
                         ).then_inc(s_zero_dma, 16)

            sp.wait_ge(mm_done[0], T0)
            sp.wait_ge(selected[0], T0 + LEAD)
            sp.dma_start(val[:, 0:FT * D], wt_d[:, :]).then_inc(s_w1t, 16)
            n = 0
            for p, tiles in enumerate(PASSES):
                for b in range(NB):
                    if n >= 2:
                        sp.wait_ge(s_base_used, n - 1)
                    sp.dma_start(base_ring[:, n % 2, :, :],
                                 bases[b, :, :].rearrange("(f p) o -> p f o", p=P)).then_inc(s_base[n % 2], 16)
                    n += 1
                    i = prev_tile(p, b - 3)
                    if i is not None:
                        sp.wait_ge(s_uev, i + 1)
                        sp.dma_start(tab1_d[P * i:P * i + ROWS[i], :], nslot(i, SLOT_U)[0:ROWS[i], :]).then_inc(s_tab1, 16)
                sp.wait_ge(s_base_used, NB * (p + 1))
                for i in tiles:
                    sp.dma_start(nslot(i, SLOT_X)[0:ROWS[i], :], x[P * i:P * i + ROWS[i], :]).then_inc(s_xre[i], 16)
            for i in PASSES[-1]:
                sp.wait_ge(s_uev, i + 1)
                sp.dma_start(tab1_d[P * i:P * i + ROWS[i], :], nslot(i, SLOT_U)[0:ROWS[i], :]).then_inc(s_tab1, 16)
            for i in range(NT):
                sp.wait_ge(s_res, i + 1)
                sp.dma_start(out[P * i:P * i + ROWS[i], :], nslot(i, SLOT_H)[0:ROWS[i], :]).then_inc(s_out, 16)
            sp.wait_ge(s_out, 16 * NT)

        @block.gpsimd
        def _(pool):
            nc.gpsimd.iota(iota_i, pattern=[[1, P]], base=0, channel_multiplier=0).then_inc(s_iota, 1)
            nc.gpsimd.iota(part_i[:, :], pattern=[[0, 1]], base=0, channel_multiplier=1).then_inc(s_iota, 1)
            nc.gpsimd.memset(past, 0.0).then_inc(s_iota, 1)
            pool.wait_ge(s_iota, 3)
            nc.gpsimd.memset(past[:, 1:2], PAD_DST).then_inc(s_rec, 1)
            pool.wait_ge(s_ident, 1)
            nc.gpsimd.tensor_copy(expand, ident[:, :].unsqueeze(2).to_broadcast([P, P, R])).then_inc(s_expand, 1)

            pool.wait_ge(s_rec_out, 32)
            pool.wait_ge(s_flag, 1)
            unsorted = pool.value_load(flag[0:1, 0:1], min_val=0, max_val=1)
            with pool.If(unsorted > 0):
                with pool.Fori(0, EC) as j:
                    pool.wait_ge(s_so_pos, j + 1)
                    pool.nop(nofuse=True)
                    pool.indirect_dma_start(
                        out=rec_d[:, :], out_offset=bass.IndirectOffsetOnAxis(ap=so_pos[:, 0:1], axis=0),
                        in_=so_rec[:, :], in_offset=None).then_inc(s_so_out, 16)
                    pool.wait_ge(s_so_out, (j + 1) * 16)
            pool.wait_ge(s_offs, 1)
            for c in range(C0 + C1):
                pool.indirect_dma_start(
                    out=padr[:, c, :, :].rearrange("p e k -> p (e k)"), out_offset=None, in_=rec_d[:, :],
                    in_offset=bass.IndirectOffsetOnAxis(ap=offs[:, c:c + 1], axis=0)).then_inc(s_padr, 16)
            pool.wait_ge(s_deg_ab, 1)
            pool.wait_ge(s_deg_out, 16)
            pool.wait_ge(s_tab0, 32)
            pool.wait_ge(s_wt_out, 16)
            nc.gpsimd.memset(flat[:, ZDMA:POOL_END], 0.0).then_inc(s_zero_pool, 1)

            def gathers(n, tab, T):
                def gather(k, i=None):
                    h = k // HALF
                    if k % HALF == 0:
                        pool.wait_ge(staged[n], h + 1 if i is None else i * 2 + (h + 1))
                    if i is not None:
                        pool.wait_ge(mm_done[n], (i - 1) * UN + (k + 1))
                        pool.nop(nofuse=True)
                    pool.indirect_dma_start(
                        out=gath[:, k, :], out_offset=None, in_=tab[:, :],
                        in_offset=bass.IndirectOffsetOnAxis(ap=stage[:, h, k % HALF:k % HALF + 1], axis=0),
                    ).then_inc(gathered[n][k], 16)

                for k in range(UN):
                    gather(k)
                with pool.Fori(1, T // UN) as i:
                    for k in range(UN):
                        gather(k, i)

            gathers(0, tab0_d, T0)
            pool.wait_ge(s_tab1, 16 * NT)
            pool.wait_ge(s_base_used, NB * len(PASSES))
            gathers(1, tab1_d, T1)

        @block.scalar
        def _(act):
            act.wait_ge(s_edges, 96)
            for k, a in enumerate((e_src, e_dst, e_typ, e_wt)):
                nc.scalar.copy(rec[:, :, k], a).then_inc(s_rec, 1)
            act.wait_ge(s_stat0, 1)
            nc.scalar.activation(rstd[:, :], mv[:, :, 1], ACT.Sqrt, bias=eps_t[:, :]).then_inc(s_sd0, 1)
            act.wait_ge(s_nmr0, 1)
            for i in range(NT):
                r = ROWS[i]
                nc.scalar.activation(x_sb[0:r, i, :], x_sb[0:r, i, :], ACT.Relu, bias=nmr[0:r, i:i + 1],
                                     scale=rstd[0:r, i:i + 1]).then_inc(s_h0, 1)
            for f in range(FT):
                act.wait_ge(s_wtr, f + 1)
                nc.scalar.copy(wt_sb[:, f, :], PS[:, 6, :]).then_inc(s_wev, 1)

            def staging(n, T, tab):
                for h in range(2):
                    nc.scalar.copy(stage[:, h, :], tab[:, HALF * h:HALF * h + HALF]).then_inc(staged[n], 1)
                with act.Fori(1, T // UN) as i:
                    for h in range(2):
                        for k in range(HALF * h, HALF * h + HALF):
                            act.wait_ge(gathered[n][k], i * 16)
                        nc.scalar.copy(stage[:, h, :], tab[:, bass.ds(i * UN + HALF * h, HALF)]).then_inc(staged[n], 1)

            act.wait_ge(s_pev, C0 + C1)
            staging(0, T0, src0)

            act.wait_ge(s_deg_in, 16)
            nc.scalar.activation(dis[:, :], dis[:, :], ACT.Sqrt).then_inc(s_deg_sqrt, 1)

            def back(g):
                if g % 2 == 0:
                    act.wait_ge(s_zt, g + 1)
                    nc.scalar.copy(Z[:, g, :], PS[:, 4 + g % 2, :]).then_inc(s_zte[0], 1)

            def keep(p):
                act.wait_ge(s_base_used, NB * (p + 1))
                for c in range(1, FT, 2):
                    for there, here in kept(p, c):
                        last = nc.scalar.copy(there, here)
                    last.then_inc(s_accfree[1], 1)

            def turned_h(i):
                r = ROWS[i]
                act.wait_ge(s_htr, i + 1)
                nc.scalar.copy(nslot(i, SLOT_HT).rearrange("p (f n) -> p f n", f=FT)[:, :, 0:r],
                               PS[:, 6, :].rearrange("p (f n) -> p f n", f=FT)[:, :, 0:r]).then_inc(s_hev, 1)

            def normalise(i):
                r = ROWS[i]
                act.wait_ge(s_stat1, i + 1)
                nc.scalar.activation(rstd[0:r, i:i + 1], mv[0:r, i, 1:2], ACT.Sqrt, bias=eps_t[0:r, :]).then_inc(s_sd1, 1)
                act.wait_ge(s_nmr1, i + 1)
                nc.scalar.activation(nslot(i, SLOT_H)[0:r, :], nslot(i, SLOT_X1)[0:r, :], ACT.Relu,
                                     bias=nmr[0:r, i:i + 1], scale=rstd[0:r, i:i + 1]).then_inc(s_h1, 1)

            for i in PASSES[0]:
                for g in GROUPS[i]:
                    back(g)
            for p in range(len(PASSES)):
                if p:
                    keep(p - 1)
                for b in range(NB):
                    if prev_tile(p, b - 1) is not None:
                        turned_h(prev_tile(p, b - 1))
                    if prev_tile(p, b) is not None:
                        normalise(prev_tile(p, b))
                    for g in later_groups(p, b):
                        back(g)
            keep(len(PASSES) - 1)
            for i in PASSES[-1]:
                normalise(i)
                turned_h(i)
            for k in range(UN):
                act.wait_ge(gathered[0][k], 16 * (T0 // UN))
            staging(1, T1, src1)
            act.wait_ge(added[1], T1)
            for i in range(NT):
                r = ROWS[i]
                nc.scalar.activation(nslot(i, SLOT_X)[0:r, :], nslot(i, SLOT_U)[0:r, :], ACT.Relu,
                                     scale=dis[0:r, i:i + 1]).then_inc(s_relu, 1)

        @block.vector
        def _(dve):
            v = nc.vector
            chain = [0]

            def link(ins):
                ins.then_inc(s_link, 1)
                chain[0] += 1
                dve.wait_ge(s_link, chain[0])

            v.memset(e_nxt, 1 << 20).then_inc(s_fill, 1)
            v.memset(ones[:, :], 1.0)
            v.memset(eps_t[:, :], EPS)
            v.memset(sel[:, :, :], 0.0).then_inc(s_zero_src, 1)
            v.memset(mv[:, :, :], 0.0)
            dve.wait_ge(s_iota, 3)
            v.tensor_copy(iota_f[:, :], iota_i)
            link(v.tensor_copy(part_f[:, :], part_i[:, :]))
            v.tensor_scalar(ident[:, :], iota_f[:, :], part_f[:, :], None, ALU.is_equal).then_inc(s_ident, 1)
            v.tensor_copy(iota_ps, iota_f[:, 0:GD])
            v.tensor_scalar(pm_i[:, 0:1], part_i[:, :], TG - 1, None, ALU.bitwise_and)
            v.tensor_scalar(pm_i[:, 1:2], part_i[:, :], 3, None, ALU.logical_shift_right)
            v.tensor_scalar(pm_i[:, 2:3], part_i[:, :], SJ - 1, None, ALU.bitwise_and)
            link(v.tensor_scalar(pm_i[:, 3:4], part_i[:, :], 1, None, ALU.logical_shift_right))
            link(v.tensor_copy(pm_f, pm_i))
            v.tensor_scalar(m_j, iota_f[:, 0:TG], pm_f[:, 0:1], None, ALU.is_equal)
            v.tensor_scalar(m_a, iota_f[:, 0:NT], pm_f[:, 1:2], None, ALU.is_equal)
            v.tensor_scalar(m_sj, iota_f[:, 0:SJ], pm_f[:, 2:3], None, ALU.is_equal)
            link(v.tensor_scalar(m_sa, iota_f[:, 0:SA], pm_f[:, 3:4], None, ALU.is_equal))

            dve.wait_ge(s_edges, 96)
            link(v.tensor_scalar(t_i, e_dst, 7, None, ALU.logical_shift_right))
            link(v.tensor_copy(ga, t_i))
            link(v.tensor_scalar(t_i, e_dst, 4, TG - 1, ALU.logical_shift_right, ALU.bitwise_and))
            link(v.tensor_copy(gb, t_i))
            for a in range(NT):
                v.tensor_scalar(oh_ga[:, a, :], ga, float(a), None, ALU.is_equal).then_inc(s_ohg, 1)
            for b in range(TG):
                v.tensor_scalar(oh_gb[:, b, :], gb, float(b), None, ALU.is_equal).then_inc(s_ohg, 1)
            link(v.tensor_tensor(viol, e_dst, e_nxt, ALU.is_gt))
            link(v.reduce_sum(viol_s, viol, AX.X))

            K = NT * TG
            dve.wait_ge(s_cnt_part, 1)
            link(v.tensor_tensor(tmp_g[0:K], PS[0:K, 0, 0:TG * TG].rearrange("p (b j) -> p b j", j=TG),
                                 m_j[0:K, :].unsqueeze(1).to_broadcast([K, TG, TG]), ALU.mult))
            link(v.reduce_sum(prt_g[0:K, :], tmp_g[0:K], AX.X))
            v.tensor_tensor(exp_g[0:K, :].rearrange("p (a b) -> p a b", a=NT),
                            prt_g[0:K, :].unsqueeze(1).to_broadcast([K, NT, TG]),
                            m_a[0:K, :].unsqueeze(2).to_broadcast([K, NT, TG]), ALU.mult).then_inc(s_exp, 1)

            dve.wait_ge(s_cnt, 1)
            v.tensor_scalar(flag[0:1, :], PS[0:1, 1, NGP:NGP + 1], 1.0, None, ALU.min).then_inc(s_flag, 1)
            link(v.tensor_copy(cnt, PS[:, 1, 0:NGP]))

            def chunks(cnt_, nch_, nch_i_, kend_, dD_, n):
                link(v.tensor_scalar(nch_i_, cnt_, float(P - 1), None, ALU.add))
                link(v.tensor_scalar(nch_i_, nch_i_, 7, None, ALU.logical_shift_right))
                link(v.tensor_copy(nch_, nch_i_))
                v.scalar_tensor_tensor(dD_, nch_, -float(P), cnt_, ALU.mult, ALU.add)
                link(v.tensor_tensor_scan(kend_, ones[:, 0:n], nch_, 0.0, ALU.mult, ALU.add))

            chunks(cnt, nch, nch_i, kend, dD, NGP)
            link(v.tensor_tensor_scan(cum, ones[:, 0:NGP], cnt, 0.0, ALU.mult, ALU.add))
            link(v.reduce_sum(cnt1, cnt.rearrange("p (a b) -> p a b", b=TG), AX.X))
            chunks(cnt1, nch1, nch1_i, kend1, dD1, NT)
            for c in range(C0 + C1):
                first, n, kend_, dD_, most, size = ((P * c, NGP, kend, dD, NG - 1, GD) if c < C0 else
                                                    (P * (c - C0), NT, kend1, dD1, NT - 1, P))
                col = slice(c, c + 1)
                link(v.tensor_scalar(tt, part_f[:, :], float(first), None, ALU.add))
                link(v.tensor_scalar(le[:, 0:n], kend_, tt, None, ALU.is_le))
                v.reduce_sum(gt[:, col], le[:, 0:n], AX.X)
                link(v.tensor_tensor(junk[:, 0:n], le[:, 0:n], dD_, ALU.mult))
                link(v.reduce_sum(oacc[:, col], junk[:, 0:n], AX.X))
                link(v.scalar_tensor_tensor(oacc[:, col], tt, float(P), oacc[:, col], ALU.mult, ALU.add))
                v.tensor_scalar(offs[:, col], oacc[:, col], float(E), None, ALU.min)
                link(v.tensor_scalar(gt[:, col], gt[:, col], float(most), None, ALU.min))
                link(v.tensor_scalar(gsc[:, col], gt[:, col], float(size), None, ALU.mult))
                if c >= C0:
                    link(v.tensor_scalar(gt[:, col], gt[:, col], float(TG), float(SLOT_U), ALU.mult, ALU.add))
            v.tensor_tensor(so_next[0:1, :], cum[0:1, :], cnt[0:1, :], ALU.subtract).then_inc(s_offs, 1)

            dve.wait_ge(s_flag, 1)
            unsorted = dve.value_load(flag[0:1, 0:1], min_val=0, max_val=1)
            with dve.If(unsorted > 0):
                v.tensor_scalar(tri, iota_f[:, :], part_f[:, :], None, ALU.is_gt)
                dve.wait_ge(s_rec, 5)
                with dve.Fori(0, EC) as j:
                    dve.wait_ge(s_so_out, j * 16)
                    v.tensor_copy(so_rec, rec[:, bass.ds(j, 1), :].rearrange("p c k -> p (c k)")).then_inc(s_so_v, 1)
                    dve.wait_ge(s_so_v, j * 7 + 1)
                    v.tensor_copy(so_dst, so_rec[:, 1:2]).then_inc(s_so_v, 1)
                    dve.wait_ge(s_so_v, j * 7 + 2)
                    v.tensor_scalar(so_dst, so_dst, 4, None, ALU.logical_shift_right).then_inc(s_so_v, 1)
                    dve.wait_ge(s_so_v, j * 7 + 3)
                    v.tensor_copy(so_grp, so_dst).then_inc(s_so_v, 1)
                    dve.wait_ge(s_so_v, j * 7 + 4)
                    v.tensor_scalar(so_oh, iota_f[0:EP, 0:NGP], so_grp, None, ALU.is_equal).then_inc(s_so_oh, 1)
                    dve.wait_ge(s_so_mm, j + 1)
                    v.tensor_tensor(so_prod, PS[0:EP, 2, 0:NGP], so_oh, ALU.mult).then_inc(s_so_v, 1)
                    v.tensor_tensor(so_next[0:1, :], PS[0:1, 3, 0:NGP], so_next[0:1, :], ALU.add).then_inc(s_so_v, 1)
                    dve.wait_ge(s_so_v, j * 7 + 6)
                    v.reduce_sum(so_posf, so_prod, AX.X).then_inc(s_so_v, 1)
                    dve.wait_ge(s_so_v, j * 7 + 7)
                    v.tensor_copy(so_pos, so_posf).then_inc(s_so_pos, 1)

            dve.wait_ge(s_xin, 32)
            for i in range(NT):
                r = ROWS[i]
                link(v.bn_stats(stats[0:r, :], x_sb[0:r, i, :]))
                link(v.bn_aggr(mv[0:r, i, :], stats[0:r, :]))
            v.memset(tt, 0.0).then_inc(s_stat0, 1)

            dve.wait_ge(s_wc, 64)
            link(v.tensor_scalar(blk_i, part_i[:, :], 5, None, ALU.logical_shift_right))
            link(v.tensor_copy(blk, blk_i))
            link(v.scalar_tensor_tensor(rel, blk, -float(R), part_f[:, :], ALU.mult, ALU.add))
            link(v.tensor_scalar(wbm, iota_f[:, 0:4], blk, None, ALU.is_equal))
            link(v.tensor_tensor(wblk, wc.unsqueeze(1).to_broadcast([P, 4, NB]),
                                 wbm.unsqueeze(2).to_broadcast([P, 4, NB]), ALU.mult))
            for s in range(3):
                part = wparts[:, s, :].rearrange("p (t b) -> p t b", b=NB)
                if s < 2:
                    link(v.tensor_copy(part, wblk))
                    link(v.tensor_tensor(wblk, wblk, part, ALU.subtract))
                else:
                    v.tensor_copy(part, wblk).then_inc(s_wparts, 1)

            dve.wait_ge(s_sd0, 1)
            link(v.reciprocal(rstd[:, :], rstd[:, :]))
            v.scalar_tensor_tensor(nmr[:, :], mv[:, :, 0], -1.0, rstd[:, :], ALU.mult, ALU.mult).then_inc(s_nmr0, 1)

            link(v.tensor_scalar(t_i, e_src, 5, None, ALU.logical_shift_right))
            link(v.tensor_copy(sa, t_i))
            link(v.tensor_scalar(t_i, e_src, SB - 1, None, ALU.bitwise_and))
            link(v.tensor_copy(sbb, t_i))
            for a in range(SA):
                v.tensor_scalar(oh_sa[:, a, :], sa, float(a), None, ALU.is_equal).then_inc(s_ohs, 1)
            for b in range(SB):
                v.tensor_scalar(oh_sb[:, b, :], sbb, float(b), None, ALU.is_equal).then_inc(s_ohs, 1)

            dve.wait_ge(s_slot_ps, 1)
            v.tensor_copy(slots[0:1, 0:T0P], PS[0:1, 2, 0:T0P])
            v.tensor_copy(slots[0:1, T0P:T0P + T1P], PS[0:1, 3, 0:T1P]).then_inc(s_slots, 1)
            K = SA * SJ
            dve.wait_ge(s_src_part, 1)
            link(v.tensor_tensor(tmp_s[0:K], PS[0:K, 0, 0:SB * SJ].rearrange("p (b j) -> p b j", j=SJ),
                                 m_sj[0:K, :].unsqueeze(1).to_broadcast([K, SB, SJ]), ALU.mult))
            v.reduce_sum(prt_s[0:K, :], tmp_s[0:K], AX.X).then_inc(s_src_masked, 1)
            dve.wait_ge(s_src_sum, 1)
            v.tensor_scalar(deg_ab[0:SA, :], PS[0:SA, 1, 0:SB], 1.0, None, ALU.add).then_inc(s_deg_ab, 1)

            dve.wait_ge(s_padr, 16 * (C0 + C1))
            for c in range(C0 + C1):
                v.tensor_scalar(padr[:, c, :, 1], padr[:, c, :, 1], gsc[:, c:c + 1], None, ALU.subtract).then_inc(s_ploc, 1)
            for c in range(C0):
                v.tensor_copy(typ16[:, c, :], padr[:, c, :, 2]).then_inc(s_ploc, 1)
            for c in range(C0 + C1):
                bank = 2 + c % 2
                dve.wait_ge(s_ptr, c + 1)
                if c < C0:
                    n = min(P, T0P - P * c)
                    v.tensor_copy(dloc0[:, P * c:P * c + n], PS[:, bank, 0:n])
                    v.tensor_copy(wtT[:, P * c:P * c + P], PS[:, bank, 2 * P:3 * P])
                    v.tensor_copy(src0[:, P * c:P * c + n], PS[:, bank, P:P + n]).then_inc(s_pev, 1)
                else:
                    a = P * (c - C0)
                    n = min(P, T1P - a)
                    v.tensor_copy(dloc1[:, a:a + n], PS[:, bank, 0:n])
                    v.tensor_copy(src1[:, a:a + n], PS[:, bank, P:P + n]).then_inc(s_pev, 1)
            dve.wait_ge(s_pev, C0 + C1)

            def value(q):
                dve.wait_ge(s_look, q + 1)
                v.tensor_tensor(val_v[:, 16 * q:16 * q + 16, :],
                                PS[:, 4 + q % 2, 0:16 * NB].rearrange("p (t b) -> p t b", b=NB),
                                wtT[:, 16 * q:16 * q + 16].unsqueeze(2).to_broadcast([P, 16, NB]),
                                ALU.mult).then_inc(s_val, 1)

            for q in range(VG):
                dve.wait_ge(s_tb, q + 1)
                if q >= 2:
                    dve.wait_ge(s_look, q - 1)
                v.tensor_scalar(oh_t[:, q % 2, :], PS[:, 2 + q % 2, :], rel, None, ALU.is_equal).then_inc(s_oht, 1)
                if q >= 1:
                    value(q - 1)
            value(VG - 1)
            dve.wait_ge(s_val, VG)
            link(v.memset(flat[:, POOL_END:NG * D], 0.0))
            dve.wait_ge(s_zero_dma, 16)
            dve.wait_ge(s_zero_pool, 1)

            def chunk_loop(n, T, select, col0):
                for t in range(LEAD):
                    select(t, t).then_inc(selected[n], 1)
                with dve.Fori(0, T // UN) as i:
                    row = nc.values_load_multi_w_load_instructions(
                        slots[0:1, bass.ds(i * UN + col0, UN)], engines=bass.OrderedEngineSet([dve.engine]),
                        min_val=0, max_val=NG - 1,
                        skip_runtime_bounds_check_because="the table's values are clamped to the last slot")[1]
                    for k in range(UN):
                        dve.wait_ge(mm_done[n], i * UN + k)
                        select(k + LEAD, i * UN + (k + LEAD)).then_inc(selected[n], 1)
                        dve.wait_ge(mm_done[n], i * UN + (k + 1))
                        dve.wait_ge(added[n], i * UN + k)
                        z = Z[:, bass.ds(row[k], 1), :].rearrange("p a d -> p (a d)")
                        v.tensor_tensor(z, z, PS[:, k % NPB, :], ALU.add).then_inc(added[n], 1)

            def col(tab, t):
                return tab[:, t:t + 1] if isinstance(t, int) else tab[:, bass.ds(t, 1)]

            def select0(k, t):
                vals = val[:, t * NB:t * NB + NB] if isinstance(t, int) else val[:, bass.ds(t * NB, NB)]
                return v.scalar_tensor_tensor(
                    sel[:, k % 4, :].rearrange("p (b d) -> p b d", b=NB), iota_ps.unsqueeze(1).to_broadcast([P, NB, GD]),
                    col(dloc0, t), vals.unsqueeze(2).to_broadcast([P, NB, GD]), ALU.is_equal, ALU.mult)

            def select1(k, t):
                return v.tensor_scalar(sel[:, k % 4, :], iota_f[:, :], col(dloc1, t), None, ALU.is_equal)

            chunk_loop(0, T0, select0, 0)

            dve.wait_ge(s_deg_sqrt, 1)
            v.reciprocal(dis[:, :], dis[:, :]).then_inc(s_dis, 1)
            dve.wait_ge(s_dis, 1)

            def back(g):
                if g % 2:
                    dve.wait_ge(s_zt, g + 1)
                    v.tensor_copy(Z[:, g, :], PS[:, 4 + g % 2, :]).then_inc(s_zte[1], 1)

            def keep(p):
                dve.wait_ge(s_base_used, NB * (p + 1))
                for c in range(0, FT, 2):
                    for there, here in kept(p, c):
                        last = v.tensor_copy(there, here)
                    last.then_inc(s_accfree[0], 1)

            def moments(i):
                r = ROWS[i]
                x1 = nslot(i, SLOT_X1)[0:r, :]
                dve.wait_ge(s_xre[i], 16)
                dve.wait_ge(s_xtr, i + 1)
                v.tensor_tensor(x1, PS[0:r, 6, :], nslot(i, SLOT_X)[0:r, :], ALU.add).then_inc(s_x1, 1)
                dve.wait_ge(s_x1, i + 1)
                v.bn_stats(stats[0:r, :], x1).then_inc(s_bn, 1)
                dve.wait_ge(s_bn, i + 1)
                v.bn_aggr(mv[0:r, i, :], stats[0:r, :]).then_inc(s_stat1, 1)
                dve.wait_ge(s_sd1, i + 1)
                v.reciprocal(rstd[0:r, i:i + 1], rstd[0:r, i:i + 1]).then_inc(s_rcp1, 1)
                dve.wait_ge(s_rcp1, i + 1)
                v.scalar_tensor_tensor(nmr[0:r, i:i + 1], mv[0:r, i, 0:1], -1.0, rstd[0:r, i:i + 1],
                                       ALU.mult, ALU.mult).then_inc(s_nmr1, 1)

            def scale_u(i):
                r = ROWS[i]
                dve.wait_ge(s_u, i + 1)
                v.tensor_scalar(nslot(i, SLOT_U)[0:r, :], PS[0:r, 7, :], dis[0:r, i:i + 1], None, ALU.mult).then_inc(s_uev, 1)

            for i in PASSES[0]:
                for g in GROUPS[i]:
                    back(g)
            for p in range(len(PASSES)):
                if p:
                    keep(p - 1)
                for b in range(NB):
                    if prev_tile(p, b - 2) is not None:
                        scale_u(prev_tile(p, b - 2))
                    if prev_tile(p, b) is not None:
                        moments(prev_tile(p, b))
                    for g in later_groups(p, b):
                        back(g)
            keep(len(PASSES) - 1)
            for i in PASSES[-1]:
                moments(i)
                scale_u(i)
            dve.wait_ge(s_uev, NT)
            chunk_loop(1, T1, select1, T0P)
            for i in range(NT):
                r = ROWS[i]
                dve.wait_ge(s_relu, i + 1)
                v.tensor_tensor(nslot(i, SLOT_H)[0:r, :], nslot(i, SLOT_X)[0:r, :], nslot(i, SLOT_X1)[0:r, :],
                                ALU.add).then_inc(s_res, 1)

        @block.tensor
        def _(pe):
            mm, tr = nc.tensor.matmul, nc.tensor.transpose
            pe.wait_ge(s_ohg, NT + TG)
            K = NT * TG
            for j in range(EC // TG):
                st = EC // TG
                last = mm(PS[0:K, 0, 0:TG * TG], flat_ga[:, j::st], flat_gb[:, j::st], start=(j == 0), stop=(j == st - 1))
            last.then_inc(s_cnt_part, 1)
            pe.wait_ge(s_exp, 1)
            mm(PS[:, 1, 0:NGP], ones[0:K, :], exp_g[0:K, :], start=True, stop=True)
            mm(PS[:, 1, NGP:NGP + 1], ones[0:EP, :], viol_s, start=True, stop=True).then_inc(s_cnt, 1)

            pe.wait_ge(s_flag, 1)
            unsorted = pe.value_load(flag[0:1, 0:1], min_val=0, max_val=1)
            with pe.If(unsorted > 0):
                with pe.Fori(0, EC) as j:
                    pe.wait_ge(s_so_oh, j + 1)
                    mm(PS[0:EP, 2, 0:NGP], tri[0:EP, 0:EP], so_oh, start=True, stop=False)
                    mm(PS[0:EP, 2, 0:NGP], ones[0:1, 0:EP], so_next[0:1, :], start=False, stop=True)
                    mm(PS[0:1, 3, 0:NGP], ones[0:EP, 0:1], so_oh, start=True, stop=True).then_inc(s_so_mm, 1)

            pe.wait_ge(s_win, 16)
            pe.wait_ge(s_ident, 1)
            for f in range(FT):
                if f:
                    pe.wait_ge(s_wev, f)
                for c in range(FT):
                    last = tr(PS[:, 6, P * c:P * (c + 1)], w_sb[:, c, P * f:P * (f + 1)], ident[:, :])
                last.then_inc(s_wtr, 1)

            pe.wait_ge(s_offs, 1)
            for c in range(C0 + C1):
                bank, at = (2, P * c) if c < C0 else (3, P * (c - C0))
                last = mm(PS[0:1, bank, at:at + P], gt[:, c:c + 1], ident[:, :], start=True, stop=True)
            last.then_inc(s_slot_ps, 1)

            pe.wait_ge(s_ohs, SA + SB)
            K = SA * SJ

            st = EC // SJ
            for j in range(st):
                last = mm(PS[0:K, 0, 0:SB * SJ], flat_sa[:, j::st], flat_sb[:, j::st], start=(j == 0), stop=(j == st - 1))
            last.then_inc(s_src_part, 1)
            pe.wait_ge(s_src_masked, 1)
            mm(PS[0:SA, 1, 0:SB], m_sa[0:K, :], prt_s[0:K, :], start=True, stop=True).then_inc(s_src_sum, 1)

            pe.wait_ge(s_slots, 1)
            pe.wait_ge(s_ploc, 2 * C0 + C1)
            for c in range(C0 + C1):
                if c >= 2:
                    pe.wait_ge(s_pev, c - 1)
                for at, field in enumerate((1, 0, 3) if c < C0 else (1, 0)):
                    last = tr(PS[:, 2 + c % 2, P * at:P * (at + 1)], padr[:, c, :, field], ident[:, :])
                last.then_inc(s_ptr, 1)
            pe.wait_ge(s_pev, C0 + C1)
            pe.wait_ge(s_expand, 1)
            pe.wait_ge(s_wparts, 1)

            def types(q):
                if q >= 2:
                    pe.wait_ge(s_oht, q - 1)
                for j in range(4):
                    t = (16 * q + 4 * j) % P
                    last = mm(PS[:, 2 + q % 2, P * j:P * (j + 1)], expand[:, t:t + 4, :], typ16[:, 16 * q // P, :],
                              start=True, stop=True)
                last.then_inc(s_tb, 1)

            def lookup(q):
                pe.wait_ge(s_oht, q + 1)
                if q >= 2:
                    pe.wait_ge(s_val, q - 1)
                for j in range(4):
                    for s in range(3):
                        last = mm(PS[:, 4 + q % 2, 4 * NB * j:4 * NB * (j + 1)], oh_t[:, q % 2, P * j:P * (j + 1)],
                                  wparts[:, s, :], start=(s == 0), stop=(s == 2))
                last.then_inc(s_look, 1)

            types(0)
            for q in range(VG):
                if q + 1 < VG:
                    types(q + 1)
                lookup(q)

            def chunk_loop(n, T):
                def chunk(k, i=None):
                    if i is None:
                        pe.wait_ge(gathered[n][k], 16)
                        pe.wait_ge(selected[n], k + 1)
                        if k >= NPB:
                            pe.wait_ge(added[n], k - NPB + 1)
                    else:
                        pe.wait_ge(gathered[n][k], i * 16 + 16)
                        pe.wait_ge(selected[n], i * UN + (k + 1))
                        pe.wait_ge(added[n], (i - 1) * UN + (k + 1 + UN - NPB))
                    mm(PS[:, k % NPB, :], sel[:, k % 4, :], gath[:, k, :], start=True, stop=True).then_inc(mm_done[n], 1)

                for k in range(UN):
                    chunk(k)
                with pe.Fori(1, T // UN) as i:
                    for k in range(UN):
                        chunk(k, i)

            pe.wait_ge(s_val, VG)
            chunk_loop(0, T0)

            def turn(g):
                if g >= 2:
                    pe.wait_ge(s_zte[g % 2], g // 2)
                for f in range(FT):
                    last = tr(PS[:, 4 + g % 2, P * f:P * (f + 1)], Z[:, g, P * f:P * (f + 1)], ident[:, :])
                last.then_inc(s_zt, 1)

            def turn_x(i):
                r = ROWS[i]
                if i == PASSES[-1][0]:
                    pe.wait_ge(s_accfree[0], 2 * len(PASSES))
                    pe.wait_ge(s_accfree[1], 2 * len(PASSES))
                if i:
                    pe.wait_ge(s_hev, i)
                for f in range(FT):
                    last = tr(PS[0:r, 6, P * f:P * (f + 1)], nslot(i, SLOT_XT)[:, P * f:P * f + r], ident[:, :])
                last.then_inc(s_xtr, 1)

            def turn_h(i):
                r = ROWS[i]
                pe.wait_ge(s_h1, i + 1)
                for f in range(FT):
                    last = tr(PS[:, 6, P * f:P * f + r], nslot(i, SLOT_H)[0:r, P * f:P * (f + 1)], ident[0:r, 0:r])
                last.then_inc(s_htr, 1)

            def project(i):
                r = ROWS[i]
                pe.wait_ge(s_hev, i + 1)
                if i:
                    pe.wait_ge(s_uev, i)
                else:
                    pe.wait_ge(s_w1t, 16)
                mm(PS[0:r, 7, :], ones[0:1, 0:r], biases[0:1, D:2 * D], start=True, stop=False)
                for f in range(FT):
                    last = mm(PS[0:r, 7, :], nslot(i, SLOT_HT)[:, P * f:P * f + r], w1t[:, f, :], start=False, stop=(f == FT - 1))
                last.then_inc(s_u, 1)

            pe.wait_ge(added[0], T0)
            pe.wait_ge(s_bias, 32)
            for i in PASSES[0]:
                for g in GROUPS[i]:
                    turn(g)
            n = 0
            for p, tiles in enumerate(PASSES):
                lastg = GROUPS[tiles[-1]][-1]
                pe.wait_ge(s_zte[0], lastg // 2 + 1)
                pe.wait_ge(s_zte[1], (lastg + 1) // 2)
                gs = [g for i in tiles for g in GROUPS[i]]
                nodes = GD * len(gs)
                for b in range(NB):
                    pe.wait_ge(s_base[n % 2], 16 * (n // 2 + 1))
                    for c in range(FT):
                        acc = PS[:, c, 0:nodes]
                        if b == 0:
                            if p:
                                pe.wait_ge(s_accfree[c % 2], 2 * (p - 1) + c // 2 + 1)
                            mm(acc, biases[0:1, P * c:P * (c + 1)], ones[0:1, 0:1].to_broadcast([1, nodes]),
                               start=True, stop=False)
                        for f in range(FT):
                            at = P * f + GD * b
                            last = mm(acc, base_ring[:, n % 2, f, P * c:P * (c + 1)],
                                      Z[:, gs[0]:gs[-1] + 1, at:at + GD],
                                      start=False, stop=(b == NB - 1 and f == FT - 1))
                    last.then_inc(s_base_used, 1)
                    n += 1
                    if prev_tile(p, b - 1) is not None:
                        turn_h(prev_tile(p, b - 1))
                    if prev_tile(p, b - 2) is not None:
                        project(prev_tile(p, b - 2))
                    if prev_tile(p, b) is not None:
                        turn_x(prev_tile(p, b))
                    for g in later_groups(p, b):
                        turn(g)
            for i in PASSES[-1]:
                turn_x(i)
                turn_h(i)
                project(i)
            chunk_loop(1, T1)


_INS = ['x', 'src', 'dst', 'edge_type_32', 'edge_weight1', 'L0_gnn_bases', 'L0_gnn_w_comp', 'L0_gnn_h_bias',
        'L1_gnn_W', 'L1_gnn_b']


def kernel(**inputs):
    import numpy as _np
    import concourse.bacc as _bacc
    from concourse import mybir as _mybir
    from concourse.bass_utils import run_bass_kernel_spmd as _run

    nc = _bacc.Bacc("TRN2", target_bir_lowering=False, num_devices=1)
    arrays, args = {}, []
    for name in _INS:
        a = _np.ascontiguousarray(inputs[name])
        arrays[f"in_{name}_dram"] = a
        args.append(nc.dram_tensor(f"in_{name}_dram", a.shape, _mybir.dt.from_np(a.dtype), kind="ExternalInput").ap())
    shape = inputs["x"].shape
    args.append(nc.dram_tensor("out_0_dram", shape, _mybir.dt.float32, kind="ExternalOutput").ap())
    gnn_kernel(nc, *args)
    r = _run(nc, [arrays], core_ids=[0])
    return r.results[0]["out_0_dram"]
```

```python
import concourse.bass as bass
from concourse import mybir
from contextlib import ExitStack


def gnn_kernel(nc, x, src, dst, etype, ew, bases, w_comp, h_bias, W1, b1, out):
    f32, bf16 = mybir.dt.float32, mybir.dt.bfloat16
    i32, u32, u16 = mybir.dt.int32, mybir.dt.uint32, mybir.dt.uint16
    ALU = mybir.AluOpType
    ACT = mybir.ActivationFunctionType
    AX = mybir.AxisListType
    P = 128

    N, D = x.shape
    E = src.shape[0]
    R, NB = w_comp.shape
    FT = D // P
    NT = -(-N // P)
    ROWS = [min(P, N - P * i) for i in range(NT)]
    GD = P // NB
    NG = -(-N // GD)
    TG = P // GD
    NGP = NT * TG
    UN = 8
    T0 = -(-((E - NG) // P + NG) // UN) * UN
    BODIES = T0 // UN
    SURE = -(-(-(-E // P)) // UN)
    C0 = -(-T0 // P)
    T0P = T0 + UN
    CW = NT * GD
    EP, EC = 125, E // 125
    assert EP * EC == E
    PAD_DST = float(1 << 20)
    EPS = 1e-5
    LEAD = 3
    NPB = 4

    rec_d = nc.dram_tensor("edge_records", [E + P, 4], f32, kind="Internal").ap()
    tab0_d = nc.dram_tensor("rows_layer0", [N, D], f32, kind="Internal").ap()
    cum_d = nc.dram_tensor("running_counts", [T0 + 1, P, CW], u16, kind="Internal").ap()
    wt_d = nc.dram_tensor("w1_transposed", [P, FT * D], f32, kind="Internal").ap()

    ctx = ExitStack()
    with ctx:
        def sb(name, shape, dt):
            return ctx.enter_context(nc.sbuf_tensor(name, shape, dt))

        def sem(name):
            return ctx.enter_context(nc.semaphore(name))

        Z = sb("Z", [P, NG, D], f32)
        gath = sb("gath", [P, UN, D], f32)
        base_ring = gath[:, :, :].rearrange("p (r f) o -> p r f o", r=2)
        sel = sb("sel", [P, 4, P], f32)
        chunk_data = sb("chunk_data", [P, T0P * (NB + 4)], f32)
        val = chunk_data[:, 0:T0P * NB]
        val_v = val.rearrange("p (t b) -> p t b", b=NB)
        dloc0, src0, negr, adx = (chunk_data[:, T0P * (NB + k):T0P * (NB + k + 1)] for k in range(4))
        src0 = src0.bitcast(u32)
        w1t = chunk_data[:, 0:FT * D].rearrange("p (f o) -> p f o", f=FT)
        biases = chunk_data[0:1, FT * D:FT * D + 2 * D]
        raw = chunk_data[:, FT * D + 2 * D:FT * D + 2 * D + (TG + 1) * CW].bitcast(u16).rearrange(
            "p (r g c) -> p r g c", r=2, c=CW)
        slots = sb("slots", [1, T0P], i32)
        ends = sb("ends", [1, NGP + 1], i32)
        stage = sb("stage", [P, 2, UN // 2], u32)
        oh_r = sb("oh_r", [P, 4, P], bf16)
        oh_ad = sb("oh_ad", [P, 4, CW], bf16)
        dist_r = sb("dist_r", [P, 2, P], bf16)
        snap = sb("snap", [P, 2, UN // 2, CW], u16)
        iota_b = sb("iota_b", [P, CW], bf16)
        ident = sb("ident", [P, P], f32)
        iota_f = sb("iota_f", [P, P], f32)
        ones = sb("ones", [P, P], f32)
        part_f = sb("part_f", [P, 1], f32)
        part_i = sb("part_i", [P, 1], i32)
        dis = sb("dis", [P, NT], f32)
        stats = sb("stats", [P, 6], f32)
        mv = sb("mv", [P, NT, 2], f32)
        rstd = sb("rstd", [P, NT], f32)
        nmr = sb("nmr", [P, NT], f32)
        eps_t = sb("eps_t", [P, 1], f32)
        flag = sb("flag", [1, 1], i32)
        bodies_t = sb("bodies_t", [1, 1], i32)

        flat = Z[:, :, :].rearrange("p g d -> p (g d)")
        early_at, late_at = [0], [64 * D]

        def words(dt, n):
            return n if dt in (f32, i32, u32) else -(-n // 2)

        def early(dt, n):
            a = early_at[0]
            early_at[0] += words(dt, n)
            assert early_at[0] <= 64 * D
            return flat[:, a:early_at[0]].bitcast(dt)

        def late(dt, n):
            a = late_at[0]
            late_at[0] += words(dt, n)
            assert late_at[0] <= NG * D
            return flat[:, a:late_at[0]].bitcast(dt)

        x_sb = early(f32, NT * D).rearrange("p (t d) -> p t d", t=NT)
        w_sb = early(f32, FT * D).rearrange("p (c i) -> p c i", c=FT)
        wt_sb = early(f32, FT * D).rearrange("p (f o) -> p f o", f=FT)
        iota_i = early(i32, CW)
        e_src, e_dst, e_typ, e_nxt = (early(i32, EC)[0:EP, :] for _ in range(4))
        e_wt = early(f32, EC)[0:EP, :]
        rec = early(f32, EC * 4)[0:EP, :].rearrange("p (c k) -> p c k", k=4)
        past = early(f32, 4)
        viol = early(f32, EC)[0:EP, :]
        viol_s = early(f32, 1)[0:EP, :]
        t_i = early(i32, EC)[0:EP, :]
        ga, gb = (early(bf16, EC)[0:EP, :] for _ in range(2))
        flat_ga, flat_gb = (early(bf16, n * EC)[0:EP, :] for n in (NT, TG))
        oh_ga, oh_gb = (a.rearrange("p (a c) -> p a c", c=EC) for a in (flat_ga, flat_gb))
        pm_i = early(i32, 4)
        pm_f = early(f32, 4)
        m_j, m_a = (early(f32, n) for n in (TG, NT))
        tmp_g = early(f32, TG * TG).rearrange("p (b j) -> p b j", b=TG)
        prt_g = early(f32, TG)
        exp_g = early(f32, NGP)
        cnt, cum, nch, kend, dD, le, junk = (early(f32, NGP) for _ in range(7))
        nch_i = early(i32, NGP)
        tt = early(f32, 1)
        gt = early(f32, C0)
        oacc = early(f32, C0)
        tri = early(f32, P)
        so_rec = early(f32, 4)[0:EP, :]
        so_dst = early(i32, 1)[0:EP, :]
        so_grp = early(f32, 1)[0:EP, :]
        so_oh = early(f32, NGP)[0:EP, :]
        so_prod = early(f32, NGP)[0:EP, :]
        so_posf = early(f32, 1)[0:EP, :]
        so_pos = early(u32, 1)[0:EP, :]
        so_next = early(f32, NGP)
        EARLY_END = early_at[0]

        offs = late(u32, C0)
        gsc = late(f32, C0)
        padr = late(f32, (C0) * P * 4).rearrange("p (c e k) -> p c e k", c=C0, k=4)
        typ16 = late(bf16, C0 * P).rearrange("p (c e) -> p c e", c=C0)
        wtT = late(f32, C0 * P)
        expand = late(bf16, P * R).rearrange("p (t r) -> p t r", r=R)
        oh_t = late(bf16, 2 * 4 * P).rearrange("p (s c) -> p s c", s=2)
        blk_i = late(i32, 1)
        part_of = late(u32, T0P)
        tile_of = late(f32, T0P)
        outside = late(f32, T0P)
        blk, rel = late(f32, 1), late(f32, 1)
        wc = late(f32, NB)
        wbm = late(f32, 4)
        wblk = late(f32, 4 * NB).rearrange("p (t b) -> p t b", t=4)
        wparts = late(bf16, 3 * 4 * NB).rearrange("p (s n) -> p s n", s=3)

        PS = ctx.enter_context(nc.psum_tensor("PS", [P, 8, D], f32))
        iota_ps = PS[:, 7, 0:GD]

        s_iota = sem("s_iota")
        s_fill = sem("s_fill")
        s_edges = sem("s_edges")
        s_xin = sem("s_xin")
        s_win = sem("s_win")
        s_wc = sem("s_wc")
        s_bias = sem("s_bias")
        s_link = sem("s_link")
        s_rec = sem("s_rec")
        s_rec_out = sem("s_rec_out")
        s_ident = sem("s_ident")
        s_ohg = sem("s_ohg")
        s_cnt_part = sem("s_cnt_part")
        s_exp = sem("s_exp")
        s_cnt = sem("s_cnt")
        s_flag = sem("s_flag")
        s_deg = sem("s_deg")
        s_deg_sqrt = sem("s_deg_sqrt")
        s_dis = sem("s_dis")
        s_bodies = sem("s_bodies")
        s_offs = sem("s_offs")
        s_slot_ps = sem("s_slot_ps")
        s_slots = sem("s_slots")
        s_padr = sem("s_padr")
        s_ploc = sem("s_ploc")
        s_ptr = sem("s_ptr")
        s_pev = sem("s_pev")
        s_expand = sem("s_expand")
        s_tb = sem("s_tb")
        s_oht = sem("s_oht")
        s_look = sem("s_look")
        s_adx = sem("s_adx")
        s_val = sem("s_val")
        s_wparts = sem("s_wparts")
        s_stat0 = sem("s_stat0")
        s_sd0 = sem("s_sd0")
        s_nmr0 = sem("s_nmr0")
        s_h0 = sem("s_h0")
        s_tab0 = sem("s_tab0")
        s_wtr = sem("s_wtr")
        s_wev = sem("s_wev")
        s_wt_out = sem("s_wt_out")
        s_zero_src = sem("s_zero_src")
        s_zero_dma = sem("s_zero_dma")
        s_zero_pool = sem("s_zero_pool")
        s_so_v = sem("s_so_v")
        s_so_oh = sem("s_so_oh")
        s_so_mm = sem("s_so_mm")
        s_so_pos = sem("s_so_pos")
        s_so_out = sem("s_so_out")
        s_staged = sem("s_staged")
        s_gathered = [sem(f"s_gathered{k}") for k in range(UN)]
        s_selected = sem("s_selected")
        s_mm = sem("s_mm")
        s_added = sem("s_added")
        s_dist = sem("s_dist")
        s_rows = sem("s_rows")
        s_counted = sem("s_counted")
        s_snap = sem("s_snap")
        s_snap_out = [sem("s_snap_out0"), sem("s_snap_out1")]
        s_base = [sem("s_base0"), sem("s_base1")]
        s_base_used = sem("s_base_used")
        s_w1t = sem("s_w1t")
        s_zt = sem("s_zt")
        s_zte = [sem("s_zt_even"), sem("s_zt_odd")]
        s_accfree = [sem("s_accfree_even"), sem("s_accfree_odd")]
        s_xtr = sem("s_xtr")
        s_xre = [sem(f"s_xre{i}") for i in range(NT)]
        s_x1 = sem("s_x1")
        s_bn = sem("s_bn")
        s_stat1 = sem("s_stat1")
        s_sd1 = sem("s_sd1")
        s_rcp1 = sem("s_rcp1")
        s_nmr1 = sem("s_nmr1")
        s_h1 = sem("s_h1")
        s_htr = sem("s_htr")
        s_hev = sem("s_hev")
        s_u = sem("s_u")
        s_uev = sem("s_uev")
        s_raw = [sem("s_raw0"), sem("s_raw1")]
        s_diff = sem("s_diff")
        s_counts = sem("s_counts")
        s_fin = sem("s_fin")
        s_relu = sem("s_relu")
        s_res = sem("s_res")
        s_out = sem("s_out")

        PASSES = [list(range(i, min(i + 4, NT))) for i in range(0, NT, 4)]
        GROUPS = [list(range(TG * i, min(TG * (i + 1), NG))) for i in range(NT)]
        VG = T0P // 16
        assert VG * 16 == T0P
        HALF = UN // 2
        ZDMA = EARLY_END // 2 // D * D
        POOL_END = 64 * D
        SLOT_X1, SLOT_U, SLOT_H, SLOT_HT, SLOT_X, SLOT_XT = range(6)

        def nslot(i, k):
            return Z[:, TG * i + k, :]

        def counts_of(j):
            home = Z[:, TG * (j // 2) + SLOT_H:TG * (j // 2) + TG, :].rearrange("p s d -> p (s d)")
            return home[:, NT * P * (j % 2):NT * P * (j % 2 + 1)].rearrange("p (a d) -> p a d", a=NT)

        def counts_step(p, b):
            j = NB * p + b - (NB + 3)
            return j if 0 <= j < NT else None

        def raw_done(j):
            return 16 * sum(len(GROUPS[i]) + 1 for i in range(j % 2, j + 1, 2))

        FBANK = [(4, 5, 0, 1, 2, 3)[j % 6] for j in range(NT)]
        BEGUN = 5

        def later_groups(p, b):
            if p + 1 == len(PASSES):
                return []
            gs = [g for i in PASSES[p + 1] for g in GROUPS[i]]
            per = -(-len(gs) // NB)
            return gs[per * b:per * (b + 1)]

        def prev_tile(p, k):
            return PASSES[p - 1][k] if p and 0 <= k < len(PASSES[p - 1]) else None

        def kept(p, c):
            tiles, ops = PASSES[p], []
            if all(r == P for r in (ROWS[i] for i in tiles)):
                there = Z[:, TG * tiles[0]:TG * (tiles[-1] + 1), :].rearrange("p (t s) d -> p t (s d)", s=TG)
                at = D * SLOT_XT + P * c
                return [(there[:, :, at:at + P], PS[:, c, 0:P * len(tiles)].rearrange("p (t n) -> p t n", n=P))]
            for k, i in enumerate(tiles):
                ops.append((nslot(i, SLOT_XT)[:, P * c:P * c + ROWS[i]], PS[:, c, P * k:P * k + ROWS[i]]))
            return ops

        def bodies_of(eng):
            eng.wait_ge(s_bodies, 1)
            return eng.value_load(bodies_t[0:1, 0:1], min_val=SURE, max_val=BODIES)

        block = ctx.enter_context(nc.Block())

        @block.sync
        def _(sp):
            sp.dma_start(e_dst, dst.rearrange("(p c) -> p c", p=EP)).then_inc(s_edges, 16)
            sp.wait_ge(s_fill, 1)
            sp.dma_start(e_nxt[0:EP - 1, :], dst[1:1 + (EP - 1) * EC].rearrange("(p c) -> p c", c=EC)).then_inc(s_edges, 16)
            sp.dma_start(e_nxt[EP - 1:EP, 0:EC - 1], dst[1 + (EP - 1) * EC:E].rearrange("(p c) -> p c", p=1)).then_inc(s_edges, 16)
            sp.dma_start(e_src, src.rearrange("(p c) -> p c", p=EP)).then_inc(s_edges, 16)
            sp.dma_start(e_typ, etype.rearrange("(p c) -> p c", p=EP)).then_inc(s_edges, 16)
            sp.dma_start(e_wt, ew.rearrange("(p c) k -> p (c k)", p=EP)).then_inc(s_edges, 16)
            full = N // P
            sp.dma_start(x_sb[:, 0:full, :], x[0:full * P, :].rearrange("(t p) d -> p t d", p=P)).then_inc(s_xin, 16)
            sp.dma_start(x_sb[0:ROWS[-1], full, :], x[full * P:N, :]).then_inc(s_xin, 16)
            for t in range(4):
                sp.dma_start(wc[R * t:R * (t + 1), :], w_comp[:, :]).then_inc(s_wc, 16)
            sp.dma_start(w_sb, W1.rearrange("(c p) i -> p c i", p=P)).then_inc(s_win, 16)
            sp.wait_ge(s_rec, 5)
            sp.dma_start(rec_d[0:E, :].rearrange("(p c) k -> p (c k)", p=EP),
                         rec.rearrange("p c k -> p (c k)")).then_inc(s_rec_out, 16)
            sp.dma_start(rec_d[E:E + P, :], past).then_inc(s_rec_out, 16)
            sp.wait_ge(s_h0, NT)
            sp.dma_start(tab0_d[0:full * P, :].rearrange("(t p) d -> p t d", p=P), x_sb[:, 0:full, :]).then_inc(s_tab0, 16)
            sp.dma_start(tab0_d[full * P:N, :], x_sb[0:ROWS[-1], full, :]).then_inc(s_tab0, 16)
            sp.wait_ge(s_wev, FT)
            sp.dma_start(wt_d[:, :], wt_sb.rearrange("p f o -> p (f o)")).then_inc(s_wt_out, 16)
            sp.wait_ge(s_tab0, 32)
            sp.wait_ge(s_wt_out, 16)
            sp.wait_ge(s_slots, 1)
            sp.wait_ge(s_zero_src, 1)
            sp.dma_start(cum_d[0, :, :], sel[:, 0, :].bitcast(u16)[:, 0:CW]).then_inc(s_zero_dma, 16)
            sp.dma_start(flat[:, 0:ZDMA].rearrange("p (n d) -> p n d", d=D),
                         sel[:, :, :].rearrange("p s c -> p (s c)").unsqueeze(1).to_broadcast([P, ZDMA // D, D])
                         ).then_inc(s_zero_dma, 16)

            def send_snaps(i):
                for h in range(2):
                    sp.wait_ge(s_snap, i * UN + HALF * (h + 1))
                    sp.dma_start(cum_d[bass.ds(i * UN + (HALF * h + 1), HALF), :, :].rearrange("t p c -> p t c"),
                                 snap[:, h, :, :]).then_inc(s_snap_out[h], 16)

            bodies = bodies_of(sp)
            with sp.Fori(0, SURE) as i:
                send_snaps(i)
            with sp.Fori(SURE, BODIES) as i:
                with sp.If(bodies > i):
                    send_snaps(i)

            sp.wait_ge(s_mm, bodies * UN)
            sp.nop(nofuse=True)
            sp.wait_ge(s_selected, bodies * UN + LEAD)
            sp.nop(nofuse=True)
            sp.wait_ge(s_rows, bodies * UN + LEAD)
            sp.nop(nofuse=True)
            sp.wait_ge(s_staged, bodies * 2 + 2)
            sp.nop(nofuse=True)
            sp.dma_start(chunk_data[:, 0:FT * D], wt_d[:, :]).then_inc(s_w1t, 16)
            sp.dma_start(biases[0:1, 0:D], h_bias.rearrange("(p d) -> p d", p=1)).then_inc(s_bias, 16)
            sp.dma_start(biases[0:1, D:2 * D], b1.rearrange("(p d) -> p d", p=1)).then_inc(s_bias, 16)
            for h in range(2):
                sp.wait_ge(s_snap_out[h], bodies * 16)
                sp.nop(nofuse=True)
            sp.wait_ge(s_zero_dma, 32)

            def raws(j):
                if j >= 2:
                    sp.wait_ge(s_diff, j - 1)
                n = len(GROUPS[j]) + 1
                row = nc.values_load_multi_w_load_instructions(
                    ends[0:1, TG * j:TG * j + n], engines=bass.OrderedEngineSet([sp.engine]), min_val=0, max_val=T0,
                    skip_runtime_bounds_check_because="a sum of chunks, of which there are at most T0")[1]
                for k in range(n):
                    sp.dma_start(raw[:, j % 2, k, :], cum_d[bass.ds(row[k], 1), :, :].rearrange("t p c -> p (t c)")
                                 ).then_inc(s_raw[j % 2], 16)

            n = 0
            for p, tiles in enumerate(PASSES):
                for b in range(NB):
                    if n >= 2:
                        sp.wait_ge(s_base_used, n - 1)
                    sp.dma_start(base_ring[:, n % 2, :, :],
                                 bases[b, :, :].rearrange("(f p) o -> p f o", p=P)).then_inc(s_base[n % 2], 16)
                    n += 1
                    if counts_step(p, b + 1) is not None:
                        raws(counts_step(p, b + 1))
                sp.wait_ge(s_base_used, NB * (p + 1))
                for i in tiles:
                    sp.dma_start(nslot(i, SLOT_X)[0:ROWS[i], :], x[P * i:P * i + ROWS[i], :]).then_inc(s_xre[i], 16)
            for i in range(NT):
                sp.wait_ge(s_res, i + 1)
                sp.dma_start(out[P * i:P * i + ROWS[i], :], nslot(i, SLOT_X1)[0:ROWS[i], :]).then_inc(s_out, 16)
            sp.wait_ge(s_out, 16 * NT)

        @block.gpsimd
        def _(pool):
            nc.gpsimd.iota(iota_i, pattern=[[1, CW]], base=0, channel_multiplier=0).then_inc(s_iota, 1)
            nc.gpsimd.iota(part_i[:, :], pattern=[[0, 1]], base=0, channel_multiplier=1).then_inc(s_iota, 1)
            nc.gpsimd.memset(past, 0.0).then_inc(s_iota, 1)
            pool.wait_ge(s_iota, 3)
            nc.gpsimd.memset(past[:, 1:2], PAD_DST).then_inc(s_rec, 1)
            pool.wait_ge(s_ident, 1)
            nc.gpsimd.tensor_copy(expand, ident[:, :].unsqueeze(2).to_broadcast([P, P, R])).then_inc(s_expand, 1)

            pool.wait_ge(s_rec_out, 32)
            pool.wait_ge(s_flag, 1)
            unsorted = pool.value_load(flag[0:1, 0:1], min_val=0, max_val=1)
            with pool.If(unsorted > 0):
                with pool.Fori(0, EC) as j:
                    pool.wait_ge(s_so_pos, j + 1)
                    pool.nop(nofuse=True)
                    pool.indirect_dma_start(
                        out=rec_d[:, :], out_offset=bass.IndirectOffsetOnAxis(ap=so_pos[:, 0:1], axis=0),
                        in_=so_rec[:, :], in_offset=None).then_inc(s_so_out, 16)
                    pool.wait_ge(s_so_out, (j + 1) * 16)
            pool.wait_ge(s_offs, 1)
            for c in range(C0):
                pool.indirect_dma_start(
                    out=padr[:, c, :, :].rearrange("p e k -> p (e k)"), out_offset=None, in_=rec_d[:, :],
                    in_offset=bass.IndirectOffsetOnAxis(ap=offs[:, c:c + 1], axis=0)).then_inc(s_padr, 16)
            pool.wait_ge(s_slots, 1)
            pool.wait_ge(s_tab0, 32)
            pool.wait_ge(s_wt_out, 16)
            nc.gpsimd.memset(flat[:, ZDMA:POOL_END], 0.0).then_inc(s_zero_pool, 1)

            def gather(k, i=None):
                h = k // HALF
                if k % HALF == 0:
                    pool.wait_ge(s_staged, h + 1 if i is None else i * 2 + (h + 1))
                if i is not None:
                    pool.wait_ge(s_mm, (i - 1) * UN + (k + 1))
                    pool.nop(nofuse=True)
                pool.indirect_dma_start(
                    out=gath[:, k, :], out_offset=None, in_=tab0_d[:, :],
                    in_offset=bass.IndirectOffsetOnAxis(ap=stage[:, h, k % HALF:k % HALF + 1], axis=0),
                ).then_inc(s_gathered[k], 16)

            for k in range(UN):
                gather(k)
            with pool.Fori(1, SURE) as i:
                for k in range(UN):
                    gather(k, i)
            bodies = bodies_of(pool)
            with pool.Fori(SURE, BODIES) as i:
                with pool.If(bodies > i):
                    for k in range(UN):
                        gather(k, i)

        @block.scalar
        def _(act):
            act.wait_ge(s_edges, 96)
            for k, a in enumerate((e_src, e_dst, e_typ, e_wt)):
                nc.scalar.copy(rec[:, :, k], a).then_inc(s_rec, 1)
            act.wait_ge(s_stat0, 1)
            nc.scalar.activation(rstd[:, :], mv[:, :, 1], ACT.Sqrt, bias=eps_t[:, :]).then_inc(s_sd0, 1)
            act.wait_ge(s_nmr0, 1)
            for i in range(NT):
                r = ROWS[i]
                nc.scalar.activation(x_sb[0:r, i, :], x_sb[0:r, i, :], ACT.Relu, bias=nmr[0:r, i:i + 1],
                                     scale=rstd[0:r, i:i + 1]).then_inc(s_h0, 1)
            for f in range(FT):
                act.wait_ge(s_wtr, f + 1)
                nc.scalar.copy(wt_sb[:, f, :], PS[:, 6, :]).then_inc(s_wev, 1)

            def rows(t, k):
                bias = negr[:, t:t + 1] if isinstance(t, int) else negr[:, bass.ds(t, 1)]
                nc.scalar.activation(dist_r[:, k % 2, :], iota_f[:, :], ACT.Abs, bias=bias, scale=1.0).then_inc(s_dist, 1)
                act.wait_ge(s_dist, t + 1)
                nc.scalar.activation(oh_r[:, k % 4, :], dist_r[:, k % 2, :], ACT.Relu, bias=1.0, scale=-1.0).then_inc(s_rows, 1)

            act.wait_ge(s_pev, C0)
            for h in range(2):
                nc.scalar.copy(stage[:, h, :], src0[:, HALF * h:HALF * h + HALF]).then_inc(s_staged, 1)
            act.wait_ge(s_adx, 1)
            for t in range(LEAD):
                rows(t, t)

            def copies(i=None):
                t0 = 0 if i is None else i * UN
                before = 0 if i is None else i * 16
                for k in range(UN):
                    h = k // HALF
                    if k or i is not None:
                        act.wait_ge(s_counted, t0 + k)
                    rows(t0 + (k + LEAD), k + LEAD)
                    if i is not None and k % HALF == 0:
                        act.wait_ge(s_snap_out[h], before)
                    act.wait_ge(s_counted, t0 + (k + 1))
                    nc.scalar.copy(snap[:, h, k % HALF, :], PS[:, 6, 0:CW]).then_inc(s_snap, 1)
                    if k % HALF == HALF - 1:
                        for q in range(HALF * h, HALF * h + HALF):
                            act.wait_ge(s_gathered[q], before + 16)
                        nc.scalar.copy(stage[:, h, :], src0[:, bass.ds(t0 + (UN + HALF * h), HALF)]).then_inc(s_staged, 1)

            copies()
            with act.Fori(1, SURE) as i:
                copies(i)
            bodies = bodies_of(act)
            with act.Fori(SURE, BODIES) as i:
                with act.If(bodies > i):
                    copies(i)

            act.wait_ge(s_deg, 1)
            nc.scalar.activation(dis[:, :], dis[:, :], ACT.Sqrt).then_inc(s_deg_sqrt, 1)

            def back(g):
                if g % 2 == 0:
                    act.wait_ge(s_zt, g + 1)
                    nc.scalar.copy(Z[:, g, :], PS[:, 4 + g % 2, :]).then_inc(s_zte[0], 1)

            def keep(p):
                act.wait_ge(s_base_used, NB * (p + 1))
                for c in range(1, FT, 2):
                    for there, here in kept(p, c):
                        last = nc.scalar.copy(there, here)
                    last.then_inc(s_accfree[1], 1)

            def turned_h(i):
                r = ROWS[i]
                act.wait_ge(s_htr, i + 1)
                nc.scalar.copy(nslot(i, SLOT_HT).rearrange("p (f n) -> p f n", f=FT)[:, :, 0:r],
                               PS[:, 6, :].rearrange("p (f n) -> p f n", f=FT)[:, :, 0:r]).then_inc(s_hev, 1)

            def normalise(i):
                r = ROWS[i]
                act.wait_ge(s_stat1, i + 1)
                nc.scalar.activation(rstd[0:r, i:i + 1], mv[0:r, i, 1:2], ACT.Sqrt, bias=eps_t[0:r, :]).then_inc(s_sd1, 1)
                act.wait_ge(s_nmr1, i + 1)
                nc.scalar.activation(nslot(i, SLOT_H)[0:r, :], nslot(i, SLOT_X1)[0:r, :], ACT.Relu,
                                     bias=nmr[0:r, i:i + 1], scale=rstd[0:r, i:i + 1]).then_inc(s_h1, 1)

            for i in PASSES[0]:
                for g in GROUPS[i]:
                    back(g)
            for p in range(len(PASSES)):
                if p:
                    keep(p - 1)
                for b in range(NB):
                    if prev_tile(p, b - 1) is not None:
                        turned_h(prev_tile(p, b - 1))
                    if prev_tile(p, b) is not None:
                        normalise(prev_tile(p, b))
                    for g in later_groups(p, b):
                        back(g)
            keep(len(PASSES) - 1)
            for i in PASSES[-1]:
                normalise(i)
                turned_h(i)
            for i in range(NT):
                r = ROWS[i]
                act.wait_ge(s_fin, i + 1)
                if i >= UN:
                    act.wait_ge(s_res, i - UN + 1)
                nc.scalar.activation(gath[0:r, i % UN, :], PS[0:r, FBANK[i], :], ACT.Relu,
                                     scale=dis[0:r, i:i + 1]).then_inc(s_relu, 1)

        @block.vector
        def _(dve):
            v = nc.vector
            chain = [0]

            def link(ins):
                ins.then_inc(s_link, 1)
                chain[0] += 1
                dve.wait_ge(s_link, chain[0])

            v.memset(e_nxt, 1 << 20).then_inc(s_fill, 1)
            v.memset(ones[:, :], 1.0)
            v.memset(eps_t[:, :], EPS)
            v.memset(sel[:, :, :], 0.0).then_inc(s_zero_src, 1)
            v.memset(mv[:, :, :], 0.0)
            dve.wait_ge(s_iota, 3)
            v.tensor_copy(iota_f[:, :], iota_i[:, 0:P])
            v.tensor_copy(iota_b[:, :], iota_i)
            link(v.tensor_copy(part_f[:, :], part_i[:, :]))
            v.tensor_scalar(ident[:, :], iota_f[:, :], part_f[:, :], None, ALU.is_equal).then_inc(s_ident, 1)
            v.tensor_copy(iota_ps, iota_f[:, 0:GD])
            v.tensor_scalar(pm_i[:, 0:1], part_i[:, :], TG - 1, None, ALU.bitwise_and)
            link(v.tensor_scalar(pm_i[:, 1:2], part_i[:, :], 3, None, ALU.logical_shift_right))
            link(v.tensor_copy(pm_f[:, 0:2], pm_i[:, 0:2]))
            v.tensor_scalar(m_j, iota_f[:, 0:TG], pm_f[:, 0:1], None, ALU.is_equal)
            link(v.tensor_scalar(m_a, iota_f[:, 0:NT], pm_f[:, 1:2], None, ALU.is_equal))

            dve.wait_ge(s_edges, 96)
            link(v.tensor_scalar(t_i, e_dst, 7, None, ALU.logical_shift_right))
            link(v.tensor_copy(ga, t_i))
            link(v.tensor_scalar(t_i, e_dst, 4, TG - 1, ALU.logical_shift_right, ALU.bitwise_and))
            link(v.tensor_copy(gb, t_i))
            for a in range(NT):
                v.tensor_scalar(oh_ga[:, a, :], ga, float(a), None, ALU.is_equal).then_inc(s_ohg, 1)
            for b in range(TG):
                v.tensor_scalar(oh_gb[:, b, :], gb, float(b), None, ALU.is_equal).then_inc(s_ohg, 1)
            link(v.tensor_tensor(viol, e_dst, e_nxt, ALU.is_gt))
            link(v.reduce_sum(viol_s, viol, AX.X))

            K = NT * TG
            dve.wait_ge(s_cnt_part, 1)
            link(v.tensor_tensor(tmp_g[0:K], PS[0:K, 0, 0:TG * TG].rearrange("p (b j) -> p b j", j=TG),
                                 m_j[0:K, :].unsqueeze(1).to_broadcast([K, TG, TG]), ALU.mult))
            link(v.reduce_sum(prt_g[0:K, :], tmp_g[0:K], AX.X))
            v.tensor_tensor(exp_g[0:K, :].rearrange("p (a b) -> p a b", a=NT),
                            prt_g[0:K, :].unsqueeze(1).to_broadcast([K, NT, TG]),
                            m_a[0:K, :].unsqueeze(2).to_broadcast([K, NT, TG]), ALU.mult).then_inc(s_exp, 1)

            dve.wait_ge(s_cnt, 1)
            v.tensor_scalar(flag[0:1, :], PS[0:1, 1, NGP:NGP + 1], 1.0, None, ALU.min).then_inc(s_flag, 1)
            link(v.tensor_copy(cnt, PS[:, 1, 0:NGP]))

            def chunks(cnt_, nch_, nch_i_, kend_, dD_, n):
                link(v.tensor_scalar(nch_i_, cnt_, float(P - 1), None, ALU.add))
                link(v.tensor_scalar(nch_i_, nch_i_, 7, None, ALU.logical_shift_right))
                link(v.tensor_copy(nch_, nch_i_))
                v.scalar_tensor_tensor(dD_, nch_, -float(P), cnt_, ALU.mult, ALU.add)
                link(v.tensor_tensor_scan(kend_, ones[:, 0:n], nch_, 0.0, ALU.mult, ALU.add))

            chunks(cnt, nch, nch_i, kend, dD, NGP)
            link(v.tensor_tensor_scan(cum, ones[:, 0:NGP], cnt, 0.0, ALU.mult, ALU.add))
            link(v.tensor_scalar(bodies_t[0:1, :], kend[0:1, NG - 1:NG], float(UN - 1), None, ALU.add))
            v.tensor_scalar(bodies_t[0:1, :], bodies_t[0:1, :], UN.bit_length() - 1, None,
                            ALU.logical_shift_right).then_inc(s_bodies, 1)
            v.memset(ends[0:1, 0:1], 0)
            v.tensor_copy(ends[0:1, 1:NGP + 1], kend[0:1, :])
            for c in range(C0):
                col = slice(c, c + 1)
                link(v.tensor_scalar(tt, part_f[:, :], float(P * c), None, ALU.add))
                link(v.tensor_scalar(le, kend, tt, None, ALU.is_le))
                v.reduce_sum(gt[:, col], le, AX.X)
                link(v.tensor_tensor(junk, le, dD, ALU.mult))
                link(v.reduce_sum(oacc[:, col], junk, AX.X))
                link(v.scalar_tensor_tensor(oacc[:, col], tt, float(P), oacc[:, col], ALU.mult, ALU.add))
                v.tensor_scalar(offs[:, col], oacc[:, col], float(E), None, ALU.min)
                link(v.tensor_scalar(gt[:, col], gt[:, col], float(NG - 1), None, ALU.min))
                link(v.tensor_scalar(gsc[:, col], gt[:, col], float(GD), None, ALU.mult))
            v.tensor_tensor(so_next[0:1, :], cum[0:1, :], cnt[0:1, :], ALU.subtract).then_inc(s_offs, 1)

            dve.wait_ge(s_flag, 1)
            unsorted = dve.value_load(flag[0:1, 0:1], min_val=0, max_val=1)
            with dve.If(unsorted > 0):
                v.tensor_scalar(tri, iota_f[:, :], part_f[:, :], None, ALU.is_gt)
                dve.wait_ge(s_rec, 5)
                with dve.Fori(0, EC) as j:
                    dve.wait_ge(s_so_out, j * 16)
                    v.tensor_copy(so_rec, rec[:, bass.ds(j, 1), :].rearrange("p c k -> p (c k)")).then_inc(s_so_v, 1)
                    dve.wait_ge(s_so_v, j * 7 + 1)
                    v.tensor_copy(so_dst, so_rec[:, 1:2]).then_inc(s_so_v, 1)
                    dve.wait_ge(s_so_v, j * 7 + 2)
                    v.tensor_scalar(so_dst, so_dst, 4, None, ALU.logical_shift_right).then_inc(s_so_v, 1)
                    dve.wait_ge(s_so_v, j * 7 + 3)
                    v.tensor_copy(so_grp, so_dst).then_inc(s_so_v, 1)
                    dve.wait_ge(s_so_v, j * 7 + 4)
                    v.tensor_scalar(so_oh, iota_f[0:EP, 0:NGP], so_grp, None, ALU.is_equal).then_inc(s_so_oh, 1)
                    dve.wait_ge(s_so_mm, j + 1)
                    v.tensor_tensor(so_prod, PS[0:EP, 2, 0:NGP], so_oh, ALU.mult).then_inc(s_so_v, 1)
                    v.tensor_tensor(so_next[0:1, :], PS[0:1, 3, 0:NGP], so_next[0:1, :], ALU.add).then_inc(s_so_v, 1)
                    dve.wait_ge(s_so_v, j * 7 + 6)
                    v.reduce_sum(so_posf, so_prod, AX.X).then_inc(s_so_v, 1)
                    dve.wait_ge(s_so_v, j * 7 + 7)
                    v.tensor_copy(so_pos, so_posf).then_inc(s_so_pos, 1)

            dve.wait_ge(s_xin, 32)
            for i in range(NT):
                r = ROWS[i]
                link(v.bn_stats(stats[0:r, :], x_sb[0:r, i, :]))
                link(v.bn_aggr(mv[0:r, i, :], stats[0:r, :]))
            v.memset(tt, 0.0).then_inc(s_stat0, 1)

            dve.wait_ge(s_wc, 64)
            link(v.tensor_scalar(blk_i, part_i[:, :], 5, None, ALU.logical_shift_right))
            link(v.tensor_copy(blk, blk_i))
            link(v.scalar_tensor_tensor(rel, blk, -float(R), part_f[:, :], ALU.mult, ALU.add))
            link(v.tensor_scalar(wbm, iota_f[:, 0:4], blk, None, ALU.is_equal))
            link(v.tensor_tensor(wblk, wc.unsqueeze(1).to_broadcast([P, 4, NB]),
                                 wbm.unsqueeze(2).to_broadcast([P, 4, NB]), ALU.mult))
            for s in range(3):
                part = wparts[:, s, :].rearrange("p (t b) -> p t b", b=NB)
                if s < 2:
                    link(v.tensor_copy(part, wblk))
                    link(v.tensor_tensor(wblk, wblk, part, ALU.subtract))
                else:
                    v.tensor_copy(part, wblk).then_inc(s_wparts, 1)

            dve.wait_ge(s_sd0, 1)
            link(v.reciprocal(rstd[:, :], rstd[:, :]))
            v.scalar_tensor_tensor(nmr[:, :], mv[:, :, 0], -1.0, rstd[:, :], ALU.mult, ALU.mult).then_inc(s_nmr0, 1)

            dve.wait_ge(s_slot_ps, 1)
            v.tensor_copy(slots[0:1, :], PS[0:1, 2, 0:T0P]).then_inc(s_slots, 1)
            dve.wait_ge(s_padr, 16 * C0)
            for c in range(C0):
                v.tensor_scalar(padr[:, c, :, 1], padr[:, c, :, 1], gsc[:, c:c + 1], None, ALU.subtract).then_inc(s_ploc, 1)
            for c in range(C0):
                v.tensor_copy(typ16[:, c, :], padr[:, c, :, 2]).then_inc(s_ploc, 1)
            for c in range(C0):
                bank = 2 + c % 2
                dve.wait_ge(s_ptr, c + 1)
                n = min(P, T0P - P * c)
                v.tensor_copy(dloc0[:, P * c:P * c + n], PS[:, bank, 0:n])
                v.tensor_copy(wtT[:, P * c:P * c + P], PS[:, bank, 2 * P:3 * P])
                v.tensor_copy(src0[:, P * c:P * c + n], PS[:, bank, P:P + n]).then_inc(s_pev, 1)
            dve.wait_ge(s_pev, C0)
            link(v.tensor_scalar(part_of, src0, P - 1, None, ALU.bitwise_and))
            link(v.tensor_scalar(negr, part_of, -1.0, None, ALU.mult))
            link(v.tensor_scalar(part_of, src0, 7, None, ALU.logical_shift_right))
            link(v.tensor_copy(tile_of, part_of))
            link(v.tensor_scalar(outside, dloc0, GD - 0.5, 1024.0, ALU.is_gt, ALU.mult))
            link(v.scalar_tensor_tensor(adx, tile_of, float(GD), dloc0, ALU.mult, ALU.add))
            v.tensor_tensor(adx, adx, outside, ALU.add).then_inc(s_adx, 1)
            dve.wait_ge(s_adx, 1)

            def value(q):
                dve.wait_ge(s_look, q + 1)
                v.tensor_tensor(val_v[:, 16 * q:16 * q + 16, :],
                                PS[:, 4 + q % 2, 0:16 * NB].rearrange("p (t b) -> p t b", b=NB),
                                wtT[:, 16 * q:16 * q + 16].unsqueeze(2).to_broadcast([P, 16, NB]),
                                ALU.mult).then_inc(s_val, 1)

            for q in range(VG):
                dve.wait_ge(s_tb, q + 1)
                if q >= 2:
                    dve.wait_ge(s_look, q - 1)
                v.tensor_scalar(oh_t[:, q % 2, :], PS[:, 2 + q % 2, :], rel, None, ALU.is_equal).then_inc(s_oht, 1)
                if q >= 1:
                    value(q - 1)
            value(VG - 1)
            dve.wait_ge(s_val, VG)
            link(v.memset(flat[:, POOL_END:NG * D], 0.0))
            dve.wait_ge(s_zero_dma, 32)
            dve.wait_ge(s_zero_pool, 1)

            def col(tab, t):
                return tab[:, t:t + 1] if isinstance(t, int) else tab[:, bass.ds(t, 1)]

            def select(k, t):
                v.tensor_scalar(oh_ad[:, k % 4, :], iota_b[:, :], col(adx, t), None, ALU.is_equal)
                vals = val[:, t * NB:t * NB + NB] if isinstance(t, int) else val[:, bass.ds(t * NB, NB)]
                v.scalar_tensor_tensor(
                    sel[:, k % 4, :].rearrange("p (b d) -> p b d", b=NB), iota_ps.unsqueeze(1).to_broadcast([P, NB, GD]),
                    col(dloc0, t), vals.unsqueeze(2).to_broadcast([P, NB, GD]), ALU.is_equal, ALU.mult
                    ).then_inc(s_selected, 1)

            for t in range(LEAD):
                select(t, t)

            def sums(i=None):
                t0 = 0 if i is None else i * UN
                row = nc.values_load_multi_w_load_instructions(
                    slots[0:1, bass.ds(t0, UN)], engines=bass.OrderedEngineSet([dve.engine]),
                    min_val=0, max_val=NG - 1,
                    skip_runtime_bounds_check_because="the table's values are clamped to the last slot")[1]
                for k in range(UN):
                    if k or i is not None:
                        dve.wait_ge(s_counted, t0 + k)
                    select(k + LEAD, t0 + (k + LEAD))
                    dve.wait_ge(s_mm, t0 + (k + 1))
                    if k or i is not None:
                        dve.wait_ge(s_added, t0 + k)
                    z = Z[:, bass.ds(row[k], 1), :].rearrange("p a d -> p (a d)")
                    v.tensor_tensor(z, z, PS[:, k % NPB, :], ALU.add).then_inc(s_added, 1)

            sums()
            with dve.Fori(1, SURE) as i:
                sums(i)
            bodies = bodies_of(dve)
            with dve.Fori(SURE, BODIES) as i:
                with dve.If(bodies > i):
                    sums(i)

            dve.wait_ge(s_snap, bodies * UN)
            link(v.reduce_sum(dis[:, :], PS[:, 6, 0:CW].rearrange("p (a d) -> p a d", a=NT), AX.X))
            v.tensor_scalar(dis[:, :], dis[:, :], 1.0, None, ALU.add).then_inc(s_deg, 1)
            dve.wait_ge(s_deg_sqrt, 1)
            v.reciprocal(dis[:, :], dis[:, :]).then_inc(s_dis, 1)
            dve.wait_ge(s_dis, 1)

            def back(g):
                if g % 2:
                    dve.wait_ge(s_zt, g + 1)
                    v.tensor_copy(Z[:, g, :], PS[:, 4 + g % 2, :]).then_inc(s_zte[1], 1)

            def keep(p):
                dve.wait_ge(s_base_used, NB * (p + 1))
                for c in range(0, FT, 2):
                    for there, here in kept(p, c):
                        last = v.tensor_copy(there, here)
                    last.then_inc(s_accfree[0], 1)

            def moments(i):
                r = ROWS[i]
                x1 = nslot(i, SLOT_X1)[0:r, :]
                dve.wait_ge(s_xre[i], 16)
                dve.wait_ge(s_xtr, i + 1)
                v.tensor_tensor(x1, PS[0:r, 6, :], nslot(i, SLOT_X)[0:r, :], ALU.add).then_inc(s_x1, 1)
                dve.wait_ge(s_x1, i + 1)
                v.bn_stats(stats[0:r, :], x1).then_inc(s_bn, 1)
                dve.wait_ge(s_bn, i + 1)
                v.bn_aggr(mv[0:r, i, :], stats[0:r, :]).then_inc(s_stat1, 1)
                dve.wait_ge(s_sd1, i + 1)
                v.reciprocal(rstd[0:r, i:i + 1], rstd[0:r, i:i + 1]).then_inc(s_rcp1, 1)
                dve.wait_ge(s_rcp1, i + 1)
                v.scalar_tensor_tensor(nmr[0:r, i:i + 1], mv[0:r, i, 0:1], -1.0, rstd[0:r, i:i + 1],
                                       ALU.mult, ALU.mult).then_inc(s_nmr1, 1)

            def scale_u(i):
                r = ROWS[i]
                dve.wait_ge(s_u, i + 1)
                v.tensor_scalar(nslot(i, SLOT_U)[0:r, :], PS[0:r, 7, :], dis[0:r, i:i + 1], None, ALU.mult).then_inc(s_uev, 1)

            def counts(j):
                n = len(GROUPS[j])
                dve.wait_ge(s_raw[j % 2], raw_done(j))
                v.tensor_tensor(counts_of(j)[:, :, 0:GD * n].rearrange("p a (g d) -> p g a d", g=n),
                                raw[:, j % 2, 1:n + 1, :].rearrange("p g (a d) -> p g a d", a=NT),
                                raw[:, j % 2, 0:n, :].rearrange("p g (a d) -> p g a d", a=NT),
                                ALU.subtract).then_inc(s_diff, 1)
                dve.wait_ge(s_diff, j + 1)
                own = counts_of(j)[:, j, 0:GD * n]
                v.tensor_tensor(own, own, ident[:, 0:GD * n], ALU.add).then_inc(s_counts, 1)

            for i in PASSES[0]:
                for g in GROUPS[i]:
                    back(g)
            for p in range(len(PASSES)):
                if p:
                    keep(p - 1)
                for b in range(NB):
                    if counts_step(p, b) is not None:
                        counts(counts_step(p, b))
                    if prev_tile(p, b - 2) is not None:
                        scale_u(prev_tile(p, b - 2))
                    if prev_tile(p, b) is not None:
                        moments(prev_tile(p, b))
                    for g in later_groups(p, b):
                        back(g)
            keep(len(PASSES) - 1)
            for i in PASSES[-1]:
                moments(i)
                scale_u(i)
            for i in range(NT):
                r = ROWS[i]
                x1 = nslot(i, SLOT_X1)[0:r, :]
                dve.wait_ge(s_relu, i + 1)
                v.tensor_tensor(x1, gath[0:r, i % UN, :], x1, ALU.add).then_inc(s_res, 1)

        @block.tensor
        def _(pe):
            mm, tr = nc.tensor.matmul, nc.tensor.transpose
            pe.wait_ge(s_ohg, NT + TG)
            K = NT * TG
            for j in range(EC // TG):
                st = EC // TG
                last = mm(PS[0:K, 0, 0:TG * TG], flat_ga[:, j::st], flat_gb[:, j::st], start=(j == 0), stop=(j == st - 1))
            last.then_inc(s_cnt_part, 1)
            pe.wait_ge(s_exp, 1)
            mm(PS[:, 1, 0:NGP], ones[0:K, :], exp_g[0:K, :], start=True, stop=True)
            mm(PS[:, 1, NGP:NGP + 1], ones[0:EP, :], viol_s, start=True, stop=True).then_inc(s_cnt, 1)

            pe.wait_ge(s_flag, 1)
            unsorted = pe.value_load(flag[0:1, 0:1], min_val=0, max_val=1)
            with pe.If(unsorted > 0):
                with pe.Fori(0, EC) as j:
                    pe.wait_ge(s_so_oh, j + 1)
                    mm(PS[0:EP, 2, 0:NGP], tri[0:EP, 0:EP], so_oh, start=True, stop=False)
                    mm(PS[0:EP, 2, 0:NGP], ones[0:1, 0:EP], so_next[0:1, :], start=False, stop=True)
                    mm(PS[0:1, 3, 0:NGP], ones[0:EP, 0:1], so_oh, start=True, stop=True).then_inc(s_so_mm, 1)

            pe.wait_ge(s_win, 16)
            pe.wait_ge(s_ident, 1)
            for f in range(FT):
                if f:
                    pe.wait_ge(s_wev, f)
                for c in range(FT):
                    last = tr(PS[:, 6, P * c:P * (c + 1)], w_sb[:, c, P * f:P * (f + 1)], ident[:, :])
                last.then_inc(s_wtr, 1)

            pe.wait_ge(s_offs, 1)
            for c in range(C0):
                last = mm(PS[0:1, 2, P * c:P * (c + 1)], gt[:, c:c + 1], ident[:, :], start=True, stop=True)
            last.then_inc(s_slot_ps, 1)

            pe.wait_ge(s_slots, 1)
            pe.wait_ge(s_ploc, 2 * C0)
            for c in range(C0):
                if c >= 2:
                    pe.wait_ge(s_pev, c - 1)
                for at, field in enumerate((1, 0, 3)):
                    last = tr(PS[:, 2 + c % 2, P * at:P * (at + 1)], padr[:, c, :, field], ident[:, :])
                last.then_inc(s_ptr, 1)
            pe.wait_ge(s_pev, C0)
            pe.wait_ge(s_expand, 1)
            pe.wait_ge(s_wparts, 1)

            def types(q):
                if q >= 2:
                    pe.wait_ge(s_oht, q - 1)
                for j in range(4):
                    t = (16 * q + 4 * j) % P
                    last = mm(PS[:, 2 + q % 2, P * j:P * (j + 1)], expand[:, t:t + 4, :], typ16[:, 16 * q // P, :],
                              start=True, stop=True)
                last.then_inc(s_tb, 1)

            def lookup(q):
                pe.wait_ge(s_oht, q + 1)
                if q >= 2:
                    pe.wait_ge(s_val, q - 1)
                for j in range(4):
                    for s in range(3):
                        last = mm(PS[:, 4 + q % 2, 4 * NB * j:4 * NB * (j + 1)], oh_t[:, q % 2, P * j:P * (j + 1)],
                                  wparts[:, s, :], start=(s == 0), stop=(s == 2))
                last.then_inc(s_look, 1)

            types(0)
            for q in range(VG):
                if q + 1 < VG:
                    types(q + 1)
                lookup(q)

            def chunk(k, i=None):
                if i is None:
                    pe.wait_ge(s_gathered[k], 16)
                    pe.wait_ge(s_selected, k + 1)
                    if k >= NPB:
                        pe.wait_ge(s_added, k - NPB + 1)
                else:
                    pe.wait_ge(s_gathered[k], i * 16 + 16)
                    pe.wait_ge(s_selected, i * UN + (k + 1))
                    pe.wait_ge(s_added, (i - 1) * UN + (k + 1 + UN - NPB))
                mm(PS[:, k % NPB, :], sel[:, k % 4, :], gath[:, k, :], start=True, stop=True).then_inc(s_mm, 1)
                first = i is None and k == 0
                if i is None:
                    pe.wait_ge(s_rows, k + 1)
                    if k:
                        pe.wait_ge(s_snap, k)
                else:
                    pe.wait_ge(s_rows, i * UN + (k + 1))
                    pe.wait_ge(s_snap, i * UN + k)
                mm(PS[:, 6, 0:CW], oh_r[:, k % 4, :], oh_ad[:, k % 4, :], start=first, stop=True,
                   skip_group_check=not first).then_inc(s_counted, 1)

            pe.wait_ge(s_val, VG)
            for k in range(UN):
                chunk(k)
            with pe.Fori(1, SURE) as i:
                for k in range(UN):
                    chunk(k, i)
            bodies = bodies_of(pe)
            with pe.Fori(SURE, BODIES) as i:
                with pe.If(bodies > i):
                    for k in range(UN):
                        chunk(k, i)

            def turn(g):
                if g >= 2:
                    pe.wait_ge(s_zte[g % 2], g // 2)
                for f in range(FT):
                    last = tr(PS[:, 4 + g % 2, P * f:P * (f + 1)], Z[:, g, P * f:P * (f + 1)], ident[:, :])
                last.then_inc(s_zt, 1)

            def turn_x(i):
                r = ROWS[i]
                if i == 0:
                    pe.wait_ge(s_deg, 1)
                if i == PASSES[-1][0]:
                    pe.wait_ge(s_accfree[0], 2 * len(PASSES))
                    pe.wait_ge(s_accfree[1], 2 * len(PASSES))
                if i:
                    pe.wait_ge(s_hev, i)
                for f in range(FT):
                    last = tr(PS[0:r, 6, P * f:P * (f + 1)], nslot(i, SLOT_XT)[:, P * f:P * f + r], ident[:, :])
                last.then_inc(s_xtr, 1)

            def turn_h(i):
                r = ROWS[i]
                pe.wait_ge(s_h1, i + 1)
                for f in range(FT):
                    last = tr(PS[:, 6, P * f:P * f + r], nslot(i, SLOT_H)[0:r, P * f:P * (f + 1)], ident[0:r, 0:r])
                last.then_inc(s_htr, 1)

            def project(i):
                r = ROWS[i]
                pe.wait_ge(s_hev, i + 1)
                if i:
                    pe.wait_ge(s_uev, i)
                else:
                    pe.wait_ge(s_w1t, 16)
                mm(PS[0:r, 7, :], ones[0:1, 0:r], biases[0:1, D:2 * D], start=True, stop=False)
                for f in range(FT):
                    last = mm(PS[0:r, 7, :], nslot(i, SLOT_HT)[:, P * f:P * f + r], w1t[:, f, :], start=False, stop=(f == FT - 1))
                last.then_inc(s_u, 1)

            pe.wait_ge(s_added, bodies * UN)
            pe.wait_ge(s_bias, 32)
            for i in PASSES[0]:
                for g in GROUPS[i]:
                    turn(g)
            n = 0
            for p, tiles in enumerate(PASSES):
                lastg = GROUPS[tiles[-1]][-1]
                pe.wait_ge(s_zte[0], lastg // 2 + 1)
                pe.wait_ge(s_zte[1], (lastg + 1) // 2)
                gs = [g for i in tiles for g in GROUPS[i]]
                nodes = GD * len(gs)
                for b in range(NB):
                    pe.wait_ge(s_base[n % 2], 16 * (n // 2 + 1))
                    for c in range(FT):
                        acc = PS[:, c, 0:nodes]
                        if b == 0:
                            if p:
                                pe.wait_ge(s_accfree[c % 2], 2 * (p - 1) + c // 2 + 1)
                            mm(acc, biases[0:1, P * c:P * (c + 1)], ones[0:1, 0:1].to_broadcast([1, nodes]),
                               start=True, stop=False)
                        for f in range(FT):
                            at = P * f + GD * b
                            last = mm(acc, base_ring[:, n % 2, f, P * c:P * (c + 1)],
                                      Z[:, gs[0]:gs[-1] + 1, at:at + GD],
                                      start=False, stop=(b == NB - 1 and f == FT - 1))
                    last.then_inc(s_base_used, 1)
                    n += 1
                    if prev_tile(p, b - 1) is not None:
                        turn_h(prev_tile(p, b - 1))
                    if prev_tile(p, b - 2) is not None:
                        project(prev_tile(p, b - 2))
                    if prev_tile(p, b) is not None:
                        turn_x(prev_tile(p, b))
                    for g in later_groups(p, b):
                        turn(g)

            def gcn(j, tiles):
                r = ROWS[j]
                if tiles[0] == 0:
                    pe.wait_ge(s_counts, j + 1)
                    if j >= 6:
                        pe.wait_ge(s_relu, j - 5)
                for a in tiles:
                    if a >= PASSES[-1][0] and j == 0:
                        pe.wait_ge(s_uev, a + 1)
                    last = mm(PS[0:r, FBANK[j], :], counts_of(j)[0:ROWS[a], a, 0:r], nslot(a, SLOT_U)[0:ROWS[a], :],
                              start=(a == 0), stop=(a == NT - 1))
                if tiles[-1] == NT - 1:
                    last.then_inc(s_fin, 1)

            early_tiles, late_tiles = list(range(PASSES[-1][0])), PASSES[-1]
            begun = 0
            for i in PASSES[-1]:
                for step in (turn_x, turn_h, project):
                    step(i)
                    if begun < BEGUN and (step is not project or i == PASSES[-1][-1]):
                        if begun == 0:
                            pe.wait_ge(s_uev, early_tiles[-1] + 1)
                        gcn(begun, early_tiles)
                        begun += 1
            for j in range(NT):
                gcn(j, late_tiles if j < begun else list(range(NT)))


_INS = ['x', 'src', 'dst', 'edge_type_32', 'edge_weight1', 'L0_gnn_bases', 'L0_gnn_w_comp', 'L0_gnn_h_bias',
        'L1_gnn_W', 'L1_gnn_b']


def kernel(**inputs):
    import numpy as _np
    import concourse.bacc as _bacc
    from concourse import mybir as _mybir
    from concourse.bass_utils import run_bass_kernel_spmd as _run

    nc = _bacc.Bacc("TRN2", target_bir_lowering=False, num_devices=1)
    arrays, args = {}, []
    for name in _INS:
        a = _np.ascontiguousarray(inputs[name])
        arrays[f"in_{name}_dram"] = a
        args.append(nc.dram_tensor(f"in_{name}_dram", a.shape, _mybir.dt.from_np(a.dtype), kind="ExternalInput").ap())
    shape = inputs["x"].shape
    args.append(nc.dram_tensor("out_0_dram", shape, _mybir.dt.float32, kind="ExternalOutput").ap())
    gnn_kernel(nc, *args)
    r = _run(nc, [arrays], core_ids=[0])
    return r.results[0]["out_0_dram"]
```

```python
import concourse.bass as bass
from concourse import mybir
from contextlib import ExitStack


def gnn_kernel(nc, x, src, dst, etype, ew, bases, w_comp, h_bias, W1, b1, out):
    f32, bf16, f16 = mybir.dt.float32, mybir.dt.bfloat16, mybir.dt.float16
    i32, u32, u16 = mybir.dt.int32, mybir.dt.uint32, mybir.dt.uint16
    ALU = mybir.AluOpType
    ACT = mybir.ActivationFunctionType
    AX = mybir.AxisListType
    P = 128

    N, D = x.shape
    E = src.shape[0]
    R, NB = w_comp.shape
    FT = D // P
    NT = -(-N // P)
    ROWS = [min(P, N - P * i) for i in range(NT)]
    GD = P // NB
    NG = -(-N // GD)
    TG = P // GD
    NGP = NT * TG
    UN = 8
    T0 = -(-((E - NG) // P + NG) // UN) * UN
    BODIES = T0 // UN
    SURE = -(-(-(-E // P)) // UN)
    C0 = -(-T0 // P)
    T0P = T0 + UN
    CW = NT * GD
    EP, EC = 125, E // 125
    assert EP * EC == E
    PAD_DST = float(1 << 20)
    EPS = 1e-5
    PIECE = 256
    PIECES = NB * FT * D // PIECE
    assert PIECES % 2 == 0 and 1 + PIECES // 2 <= SURE
    LEAD = 3
    NPB = 4

    rec_d = nc.dram_tensor("edge_records", [E + P, 4], f32, kind="Internal").ap()
    tab0_d = nc.dram_tensor("rows_layer0", [N, D], f32, kind="Internal").ap()
    cum_d = nc.dram_tensor("running_counts", [T0 + 1, P, CW], u16, kind="Internal").ap()
    parts_d = nc.dram_tensor("bases_parts", [NB, P, 2 * FT * D], f16, kind="Internal").ap()
    wt_d = nc.dram_tensor("w1_transposed", [P, FT * D], f32, kind="Internal").ap()

    ctx = ExitStack()
    with ctx:
        def sb(name, shape, dt):
            return ctx.enter_context(nc.sbuf_tensor(name, shape, dt))

        def sem(name):
            return ctx.enter_context(nc.semaphore(name))

        Z = sb("Z", [P, NG, D], f32)
        gath = sb("gath", [P, UN, D], f32)
        base_ring = gath[:, :, :].rearrange("p k d -> p (k d)").bitcast(f16).rearrange(
            "p (r s f o) -> p r s f o", r=2, s=2, f=FT)
        sel = sb("sel", [P, 4, P], f32)
        chunk_data = sb("chunk_data", [P, T0P * (NB + 4)], f32)
        val = chunk_data[:, 0:T0P * NB]
        val_v = val.rearrange("p (t b) -> p t b", b=NB)
        dloc0, src0, src_in, neg_col = (chunk_data[:, T0P * (NB + k):T0P * (NB + k + 1)] for k in range(4))
        src0 = src0.bitcast(u32)
        whole = chunk_data[:, 0:FT * D].rearrange("p (h n) -> p h n", h=2)
        raw = chunk_data[:, 0:(TG + 1) * CW].bitcast(u16).rearrange("p (r g c) -> p r g c", r=2, c=CW)
        w1t = chunk_data[:, FT * D:2 * FT * D].bitcast(f16).rearrange("p (s f o) -> p s f o", s=2, f=FT)
        gained = chunk_data[:, 2 * FT * D:2 * FT * D + NT * P // 2].bitcast(u16).rearrange("p (a d) -> p a d", a=NT)
        slots = sb("slots", [1, T0P], i32)
        ends = sb("ends", [1, NGP + 1], i32)
        stage = sb("stage", [P, 2, UN // 2], u32)
        oh_r = sb("oh_r", [P, 4, P], bf16)
        oh_ad = sb("oh_ad", [P, 4, CW], bf16)
        dist = sb("dist", [P, 2, CW], bf16)
        snap = sb("snap", [P, 2, UN // 2, CW], u16)
        hb_t = sel[:, :, :].rearrange("p s c -> p (s c)")
        b1_t = snap[:, :, :, :].rearrange("p h k c -> p (h k c)").bitcast(f32)[:, 0:D]
        iota_b = sb("iota_b", [P, CW], bf16)
        ident = sb("ident", [P, P], f32)
        iota_f = sb("iota_f", [P, P], f32)
        ones = sb("ones", [P, P], f32)
        part_f = sb("part_f", [P, 1], f32)
        part_i = sb("part_i", [P, 1], i32)
        dis = sb("dis", [P, NT], f32)
        stats = sb("stats", [P, 6], f32)
        mv = sb("mv", [P, NT, 2], f32)
        rstd = sb("rstd", [P, NT], f32)
        nmr = sb("nmr", [P, NT], f32)
        eps_t = sb("eps_t", [P, 1], f32)
        flag = sb("flag", [1, 1], i32)
        big_t = sb("big_t", [1, 1], i32)
        SQ_EW, SQ_WC, SQ_W, SQ_B, SQ_BASE, NSQ = range(6)
        piece = sb("piece", [P, PIECE], f32)
        sq_piece = sb("sq_piece", [P, PIECES], f32)
        sq = sb("sq", [P, NSQ], f32)
        sq_max = sb("sq_max", [P, 1], f32)
        sq_all = sb("sq_all", [P, NSQ], f32)
        sq_diag = sb("sq_diag", [P, NSQ], f32)
        SC_BASE, SC_W, SC_U, NSC = NGP, NGP + 1, NGP + 2, NGP + 3
        bound = sb("bound", [P, NSC], f32)
        half_e = sb("half_e", [P, NSC], i32)
        scale_i = sb("scale_i", [P, NSC], i32)
        unscale_i = sb("unscale_i", [P, NSC], i32)
        scale, unscale = scale_i[:, :].bitcast(f32), unscale_i[:, :].bitcast(f32)
        m_g = sb("m_g", [P, TG], f32)
        unscale_g = bound[:, 0:NGP]
        unscale_n = sb("unscale_n", [P, NT], f32)
        dis_up = sb("dis_up", [P, NT], f32)
        bodies_t = sb("bodies_t", [1, 1], i32)

        flat = Z[:, :, :].rearrange("p g d -> p (g d)")
        LATE_AT = 60 * D
        early_at, late_at = [0], [LATE_AT]

        def words(dt, n):
            return n if dt in (f32, i32, u32) else -(-n // 2)

        def early(dt, n):
            a = early_at[0]
            early_at[0] += words(dt, n)
            assert early_at[0] <= LATE_AT
            return flat[:, a:early_at[0]].bitcast(dt)

        def late(dt, n):
            a = late_at[0]
            late_at[0] += words(dt, n)
            assert late_at[0] <= NG * D
            return flat[:, a:late_at[0]].bitcast(dt)

        x_rest = early(f32, (NT - UN) * D).rearrange("p (t d) -> p t d", t=NT - UN)
        w_sb = early(f32, FT * D).rearrange("p (c i) -> p c i", c=FT)
        wt_sb = early(f32, FT * D).rearrange("p (f o) -> p f o", f=FT)
        iota_i = early(i32, CW)
        e_src, e_dst, e_typ, e_nxt = (early(i32, EC)[0:EP, :] for _ in range(4))
        e_wt = early(f32, EC)[0:EP, :]
        rec = early(f32, EC * 4)[0:EP, :].rearrange("p (c k) -> p c k", k=4)
        past = early(f32, 4)
        viol = early(f32, EC)[0:EP, :]
        viol_s = early(f32, 1)[0:EP, :]
        t_i = early(i32, EC)[0:EP, :]
        ga, gb = (early(bf16, EC)[0:EP, :] for _ in range(2))
        flat_ga, flat_gb = (early(bf16, n * EC)[0:EP, :] for n in (NT, TG))
        oh_ga, oh_gb = (a.rearrange("p (a c) -> p a c", c=EC) for a in (flat_ga, flat_gb))
        pm_i = early(i32, 4)
        pm_f = early(f32, 4)
        squares = early(f32, FT * D)
        b_row = early(f32, D)[0:1, :]
        m_j, m_a = (early(f32, n) for n in (TG, NT))
        tmp_g = early(f32, TG * TG).rearrange("p (b j) -> p b j", b=TG)
        prt_g = early(f32, TG)
        exp_g = early(f32, NGP)
        cnt, cum, nch, kend, dD = (early(f32, NGP) for _ in range(5))
        le, junk = (early(f32, C0 * NGP).rearrange("p (c g) -> p c g", c=C0) for _ in range(2))
        nch_i = early(i32, NGP)
        tt = early(f32, C0)
        gt = early(f32, C0)
        oacc = early(f32, C0)
        tri = early(f32, P)
        so_rec = early(f32, 4)[0:EP, :]
        so_dst = early(i32, 1)[0:EP, :]
        so_grp = early(f32, 1)[0:EP, :]
        so_oh = early(f32, NGP)[0:EP, :]
        so_prod = early(f32, NGP)[0:EP, :]
        so_posf = early(f32, 1)[0:EP, :]
        so_pos = early(u32, 1)[0:EP, :]
        so_next = early(f32, NGP)
        EARLY_END = early_at[0]

        typ16 = late(bf16, C0 * P).rearrange("p (c e) -> p c e", c=C0)
        expand = late(bf16, P * R).rearrange("p (t r) -> p t r", r=R)
        LOOK_AT = -(-late_at[0] // D) * D
        late_at[0] = LOOK_AT
        wtT = late(f32, C0 * P)
        types_b = late(bf16, 3 * 4 * P).rearrange("p (s c) -> p s c", s=3)
        oh_t = late(bf16, 2 * 4 * P).rearrange("p (s c) -> p s c", s=2)
        rel = late(f32, 1)
        wparts = late(bf16, 3 * 4 * NB).rearrange("p (s n) -> p s n", s=3)
        MID_AT = -(-late_at[0] // D) * D
        late_at[0] = MID_AT
        offs = late(u32, C0)
        gsc = late(f32, C0)
        padr = late(f32, C0 * P * 4).rearrange("p (c e k) -> p c e k", c=C0, k=4)
        blk_i = late(i32, 1)
        part_of = late(u32, T0P)
        tile_of = late(f32, T0P)
        outside = late(f32, T0P)
        blk = late(f32, 1)
        wc = late(f32, NB)
        wbm = late(f32, 4)
        wblk = late(f32, 4 * NB).rearrange("p (t b) -> p t b", t=4)

        PS = ctx.enter_context(nc.psum_tensor("PS", [P, 8, D], f32))
        iota_ps = PS[:, 7, 0:GD]

        def x_tile(i):
            return (gath[:, i, :] if i < UN else x_rest[:, i - UN, :])[0:ROWS[i], :]

        s_iota = sem("s_iota")
        s_fill = sem("s_fill")
        s_edges = sem("s_edges")
        s_xin = sem("s_xin")
        s_win = sem("s_win")
        s_wc = sem("s_wc")
        s_bias = sem("s_bias")
        s_link = sem("s_link")
        s_rec = sem("s_rec")
        s_rec_out = sem("s_rec_out")
        s_ident = sem("s_ident")
        s_ohg = sem("s_ohg")
        s_cnt_part = sem("s_cnt_part")
        s_exp = sem("s_exp")
        s_cnt = sem("s_cnt")
        s_flag = sem("s_flag")
        s_deg = sem("s_deg")
        s_deg_sqrt = sem("s_deg_sqrt")
        s_dis = sem("s_dis")
        s_bodies = sem("s_bodies")
        s_offs = sem("s_offs")
        s_table = sem("s_table")
        s_slot_ps = sem("s_slot_ps")
        s_slots = sem("s_slots")
        s_sq = sem("s_sq")
        s_sq0 = sem("s_sq0")
        s_sq_zero = sem("s_sq_zero")
        s_piece = sem("s_piece")
        s_brow = sem("s_brow")
        s_sqt = [sem("s_sqt0"), sem("s_sqt1")]
        s_sqd = [sem("s_sqd0"), sem("s_sqd1")]
        s_sqall = [sem("s_sqall0"), sem("s_sqall1")]
        s_scale = [sem("s_scale0"), sem("s_scale1")]
        s_node = sem("s_node")
        s_whole = [sem("s_whole0"), sem("s_whole1")]
        s_whi = sem("s_whi")
        s_wlo = sem("s_wlo")
        s_parts_out = [sem("s_parts_out0"), sem("s_parts_out1")]
        s_padr = sem("s_padr")
        s_ploc = sem("s_ploc")
        s_ptr = sem("s_ptr")
        s_pev = sem("s_pev")
        s_expand = sem("s_expand")
        s_tb = sem("s_tb")
        s_oht = sem("s_oht")
        s_types = sem("s_types")
        s_look = sem("s_look")
        s_cols = sem("s_cols")
        s_val = sem("s_val")
        s_wparts = sem("s_wparts")
        s_stat0 = sem("s_stat0")
        s_sd0 = sem("s_sd0")
        s_nmr0 = sem("s_nmr0")
        s_h0 = sem("s_h0")
        s_tab0 = sem("s_tab0")
        s_wtr = sem("s_wtr")
        s_wev = sem("s_wev")
        s_wt_out = sem("s_wt_out")
        s_zero_src = sem("s_zero_src")
        s_zero_dma = sem("s_zero_dma")
        s_zero_pool = sem("s_zero_pool")
        s_so_v = sem("s_so_v")
        s_so_oh = sem("s_so_oh")
        s_so_mm = sem("s_so_mm")
        s_so_pos = sem("s_so_pos")
        s_so_out = sem("s_so_out")
        s_staged = sem("s_staged")
        s_gathered = [sem(f"s_gathered{k}") for k in range(UN)]
        s_selected = sem("s_selected")
        s_mm = sem("s_mm")
        s_added = sem("s_added")
        s_dist = sem("s_dist")
        s_rows = sem("s_rows")
        s_counted = sem("s_counted")
        s_snap = sem("s_snap")
        s_snap_out = [sem("s_snap_out0"), sem("s_snap_out1")]
        s_base = [sem("s_base0"), sem("s_base1")]
        s_base_sq = sem("s_base_sq")
        s_base_used = sem("s_base_used")
        s_zt = sem("s_zt")
        s_zhi = sem("s_zhi")
        s_zlo = sem("s_zlo")
        s_accfree = [sem("s_accfree_even"), sem("s_accfree_odd")]
        s_xtr = sem("s_xtr")
        s_xre = [sem(f"s_xre{i}") for i in range(NT)]
        s_x1 = sem("s_x1")
        s_bn = sem("s_bn")
        s_stat1 = sem("s_stat1")
        s_sd1 = sem("s_sd1")
        s_rcp1 = sem("s_rcp1")
        s_nmr1 = sem("s_nmr1")
        s_h1 = sem("s_h1")
        s_htr = sem("s_htr")
        s_hhi = sem("s_hhi")
        s_hlo = sem("s_hlo")
        s_u = sem("s_u")
        s_ub = sem("s_ub")
        s_uhi = sem("s_uhi")
        s_xb = sem("s_xb")
        s_split = sem("s_split")
        s_big = sem("s_big")
        s_big_t = sem("s_big_t")
        s_uev = sem("s_uev")
        s_raw = [sem("s_raw0"), sem("s_raw1")]
        s_diff = sem("s_diff")
        s_rest = sem("s_rest")
        s_counts = sem("s_counts")
        s_fin = sem("s_fin")
        s_relu = sem("s_relu")
        s_res = sem("s_res")
        s_out = sem("s_out")

        PASSES = [list(range(i, min(i + 4, NT))) for i in range(0, NT, 4)]
        GROUPS = [list(range(TG * i, min(TG * (i + 1), NG))) for i in range(NT)]
        VG = T0P // 16
        assert VG * 16 == T0P
        HALF = UN // 2
        XEARLY = 6
        LN_AT = NT - XEARLY + 1
        DIRECT = range(LN_AT, LN_AT + 9)
        ZPOOL = -(-EARLY_END // D) * D
        ZDMA = (NT - UN + 2 * FT) * D
        SLOT_X1, SLOT_U, SLOT_H, SLOT_HT, SLOT_X, SLOT_XT = range(6)

        def nslot(i, k):
            return Z[:, TG * i + k, :]

        def counts_of(j, s=0):
            home = Z[:, TG * (j // 2) + SLOT_H:TG * (j // 2) + TG, :].rearrange("p s d -> p (s d)").bitcast(f16)
            at = NT * P * (2 * (j % 2) + s)
            return home[:, at:at + NT * P].rearrange("p (a d) -> p a d", a=NT)

        def parts(i, k, s):
            return nslot(i, k).bitcast(f16)[:, D * s:D * (s + 1)]

        def zparts(g, s):
            return Z[:, g, :].bitcast(f16)[:, D * s:D * (s + 1)]

        FIRST = sum(len(GROUPS[i]) for i in PASSES[0])

        def zbank(g):
            return g % 4 if g < FIRST else 4 + g % 2

        def zbank_before(g):
            return max([q + 1 for q in range(g) if zbank(q) == zbank(g)], default=0)

        def counts_step(p, b):
            j = NB * p + b - (NB + 3)
            return j if 0 <= j < NT else None

        def raw_done(j):
            return 16 * sum(len(GROUPS[i]) + 1 for i in range(j % 2, j + 1, 2))

        FBANK = [(4, 5, 0, 1, 2, 3)[j % 6] for j in range(NT)]
        BEGUN = 5

        def later_groups(p, b):
            if p + 1 == len(PASSES):
                return []
            gs = [g for i in PASSES[p + 1] for g in GROUPS[i]]
            per = -(-len(gs) // NB)
            return gs[per * b:per * (b + 1)]

        def prev_tile(p, k):
            return PASSES[p - 1][k] if p and 0 <= k < len(PASSES[p - 1]) else None

        def kept(p, c):
            tiles, ops = PASSES[p], []
            if all(r == P for r in (ROWS[i] for i in tiles)):
                there = Z[:, TG * tiles[0]:TG * (tiles[-1] + 1), :].rearrange("p (t s) d -> p t (s d)", s=TG)
                at = D * SLOT_XT + P * c
                return [(there[:, :, at:at + P], PS[:, c, 0:P * len(tiles)].rearrange("p (t n) -> p t n", n=P))]
            for k, i in enumerate(tiles):
                ops.append((nslot(i, SLOT_XT)[:, P * c:P * c + ROWS[i]], PS[:, c, P * k:P * k + ROWS[i]]))
            return ops

        def bodies_of(eng):
            eng.wait_ge(s_bodies, 1)
            return eng.value_load(bodies_t[0:1, 0:1], min_val=SURE, max_val=BODIES)

        block = ctx.enter_context(nc.Block())

        @block.sync
        def _(sp):
            sp.dma_start(e_dst, dst.rearrange("(p c) -> p c", p=EP)).then_inc(s_edges, 16)
            sp.wait_ge(s_fill, 1)
            sp.dma_start(e_nxt[0:EP - 1, :], dst[1:1 + (EP - 1) * EC].rearrange("(p c) -> p c", c=EC)).then_inc(s_edges, 16)
            sp.dma_start(e_nxt[EP - 1:EP, 0:EC - 1], dst[1 + (EP - 1) * EC:E].rearrange("(p c) -> p c", p=1)).then_inc(s_edges, 16)
            sp.dma_start(e_src, src.rearrange("(p c) -> p c", p=EP)).then_inc(s_edges, 16)
            sp.dma_start(e_typ, etype.rearrange("(p c) -> p c", p=EP)).then_inc(s_edges, 16)
            sp.dma_start(e_wt, ew.rearrange("(p c) k -> p (c k)", p=EP)).then_inc(s_edges, 16)
            sp.dma_start(gath[:, :, :], x[0:UN * P, :].rearrange("(t p) d -> p t d", p=P)).then_inc(s_xin, 16)
            for i in range(UN, NT):
                sp.dma_start(x_tile(i), x[P * i:P * i + ROWS[i], :]).then_inc(s_xin, 16)
            for t in range(4):
                sp.dma_start(wc[R * t:R * (t + 1), :], w_comp[:, :]).then_inc(s_wc, 16)
            sp.dma_start(w_sb, W1.rearrange("(c p) i -> p c i", p=P)).then_inc(s_win, 16)
            sp.dma_start(b_row, b1.rearrange("(p d) -> p d", p=1)).then_inc(s_brow, 16)
            sp.wait_ge(s_rec, 5)
            sp.dma_start(rec_d[0:E, :].rearrange("(p c) k -> p (c k)", p=EP),
                         rec.rearrange("p c k -> p (c k)")).then_inc(s_rec_out, 16)
            sp.dma_start(rec_d[E:E + P, :], past).then_inc(s_rec_out, 16)
            sp.wait_ge(s_wev, FT)
            sp.dma_start(wt_d[:, :], wt_sb.rearrange("p f o -> p (f o)")).then_inc(s_wt_out, 16)
            sp.wait_ge(s_wt_out, 16)
            sp.wait_ge(s_slots, 1)
            sp.wait_ge(s_sq0, 4)
            sp.wait_ge(s_zero_src, 1)
            sp.dma_start(cum_d[0, :, :], snap[:, 0, 0, :]).then_inc(s_zero_dma, 16)

            def zero(a, b):
                sp.dma_start(flat[:, a:b].rearrange("p (n d) -> p n d", d=D),
                             snap[:, :, :, :].rearrange("p h k c -> p (h k c)").bitcast(f32)[:, 0:D].unsqueeze(1)
                             .to_broadcast([P, (b - a) // D, D])).then_inc(s_zero_dma, 16)

            zero((NT - UN) * D, ZDMA)
            sp.wait_ge(s_cols, 1)
            zero(MID_AT, NG * D)
            sp.wait_ge(s_h0, NT)
            sp.dma_start(tab0_d[0:UN * P, :].rearrange("(t p) d -> p t d", p=P), gath[:, :, :]).then_inc(s_tab0, 16)
            for i in range(UN, NT):
                sp.dma_start(tab0_d[P * i:P * i + ROWS[i], :], x_tile(i)).then_inc(s_tab0, 16)
            sp.wait_ge(s_tab0, 16 * (NT - UN + 1))
            zero(0, (NT - UN) * D)
            sp.wait_ge(s_tb, VG)
            zero(LATE_AT, LOOK_AT)

            pieces_d = bases.rearrange("b i o -> (b i o)").rearrange("(n p o) -> n p o", p=P, o=PIECE)

            def send_snaps(i, n=None):
                for h in range(2):
                    if n is not None:
                        if h or not isinstance(n, int):
                            sp.wait_ge(s_sq, n + h)
                            sp.nop(nofuse=True)
                        sp.dma_start(piece[:, :], pieces_d[bass.ds(n + h, 1), :, :].rearrange("t p o -> p (t o)")
                                     ).then_inc(s_piece, 16)
                    sp.wait_ge(s_snap, i * UN + HALF * (h + 1))
                    sp.dma_start(cum_d[bass.ds(i * UN + (HALF * h + 1), HALF), :, :].rearrange("t p c -> p t c"),
                                 snap[:, h, :, :]).then_inc(s_snap_out[h], 16)

            bodies = bodies_of(sp)
            send_snaps(0, 0)
            with sp.Fori(1, PIECES // 2) as i:
                send_snaps(i, i * 2)
            with sp.Fori(PIECES // 2, SURE) as i:
                send_snaps(i)
            with sp.Fori(SURE, BODIES) as i:
                with sp.If(bodies > i):
                    send_snaps(i)

            sp.wait_ge(s_mm, bodies * UN)
            sp.nop(nofuse=True)
            sp.wait_ge(s_selected, bodies * UN + LEAD)
            sp.nop(nofuse=True)
            sp.wait_ge(s_rows, bodies * UN + LEAD)
            sp.nop(nofuse=True)
            sp.wait_ge(s_staged, bodies * 2 + 2)
            sp.nop(nofuse=True)
            for h in range(2):
                sp.wait_ge(s_snap_out[h], bodies * 16)
                sp.nop(nofuse=True)

            def load_whole(n):
                for h in range(2):
                    if n:
                        sp.wait_ge(s_wlo, 2 * (n - 1) + h + 1)
                    there = whole[:, h, :]
                    if n < NB:
                        sp.dma_start(there.rearrange("p (f o) -> p f o", o=D),
                                     bases[n, P * FT // 2 * h:P * FT // 2 * (h + 1), :].rearrange("(f p) o -> p f o", p=P)
                                     ).then_inc(s_whole[h], 16)
                    else:
                        sp.dma_start(there, wt_d[:, FT * D // 2 * h:FT * D // 2 * (h + 1)]).then_inc(s_whole[h], 16)

            def store_parts(n):
                sp.wait_ge(s_wlo, 2 * n + 2)
                sp.dma_start(parts_d[n, :, :], base_ring[:, n % 2, :, :, :].rearrange("p s f o -> p (s f o)")
                             ).then_inc(s_parts_out[n % 2], 16)

            load_whole(0)
            sp.dma_start(hb_t, h_bias.rearrange("(p d) -> p d", p=1).to_broadcast([P, D])).then_inc(s_bias, 16)
            sp.dma_start(b1_t, b1.rearrange("(p d) -> p d", p=1).to_broadcast([P, D])).then_inc(s_bias, 16)

            def raws(j):
                if j >= 2:
                    sp.wait_ge(s_counts, j - 1)
                n = len(GROUPS[j]) + 1
                row = nc.values_load_multi_w_load_instructions(
                    ends[0:1, TG * j:TG * j + n], engines=bass.OrderedEngineSet([sp.engine]), min_val=0, max_val=T0,
                    skip_runtime_bounds_check_because="a sum of chunks, of which there are at most T0")[1]
                for k in range(n):
                    sp.dma_start(raw[:, j % 2, k, :], cum_d[bass.ds(row[k], 1), :, :].rearrange("t p c -> p (t c)")
                                 ).then_inc(s_raw[j % 2], 16)

            for b in range(NB):
                if b + 1 < NB:
                    load_whole(b + 1)
                store_parts(b)
            n = NB
            for p, tiles in enumerate(PASSES):
                for b in range(NB if p else 0):
                    sp.wait_ge(s_base_used, n - 1)
                    if b == 1:
                        for i in PASSES[p - 1]:
                            sp.dma_start(nslot(i, SLOT_X)[0:ROWS[i], :], x[P * i:P * i + ROWS[i], :]).then_inc(s_xre[i], 16)
                    if p == 1 and b < 2:
                        sp.wait_ge(s_parts_out[b % 2], 16 * NB // 2)
                    sp.dma_start(base_ring[:, n % 2, :, :, :].rearrange("p s f o -> p (s f o)"),
                                 parts_d[b, :, :]).then_inc(s_base[n % 2], 16)
                    n += 1
                    if p == 1 and b == 1:
                        load_whole(NB)
                    if counts_step(p, b + 1) is not None:
                        if counts_step(p, b + 1) == 0:
                            sp.wait_ge(s_wlo, 2 * NB + 2)
                        raws(counts_step(p, b + 1))
            sp.wait_ge(s_base_used, NB * len(PASSES))
            for i in PASSES[-1]:
                sp.dma_start(nslot(i, SLOT_X)[0:ROWS[i], :], x[P * i:P * i + ROWS[i], :]).then_inc(s_xre[i], 16)
            for i in range(NT):
                sp.wait_ge(s_res, i + 1)
                sp.dma_start(out[P * i:P * i + ROWS[i], :], nslot(i, SLOT_X1)[0:ROWS[i], :]).then_inc(s_out, 16)
            sp.wait_ge(s_out, 16 * NT)

        @block.gpsimd
        def _(pool):
            nc.gpsimd.iota(iota_i, pattern=[[1, CW]], base=0, channel_multiplier=0).then_inc(s_iota, 1)
            nc.gpsimd.iota(part_i[:, :], pattern=[[0, 1]], base=0, channel_multiplier=1).then_inc(s_iota, 1)
            nc.gpsimd.memset(past, 0.0).then_inc(s_iota, 1)
            pool.wait_ge(s_iota, 3)
            nc.gpsimd.memset(past[:, 1:2], PAD_DST).then_inc(s_rec, 1)
            pool.wait_ge(s_ident, 1)
            nc.gpsimd.tensor_copy(expand, ident[:, :].unsqueeze(2).to_broadcast([P, P, R])).then_inc(s_expand, 1)

            pool.wait_ge(s_rec_out, 32)
            pool.wait_ge(s_flag, 1)
            unsorted = pool.value_load(flag[0:1, 0:1], min_val=0, max_val=1)
            with pool.If(unsorted > 0):
                with pool.Fori(0, EC) as j:
                    pool.wait_ge(s_so_pos, j + 1)
                    pool.nop(nofuse=True)
                    pool.indirect_dma_start(
                        out=rec_d[:, :], out_offset=bass.IndirectOffsetOnAxis(ap=so_pos[:, 0:1], axis=0),
                        in_=so_rec[:, :], in_offset=None).then_inc(s_so_out, 16)
                    pool.wait_ge(s_so_out, (j + 1) * 16)
            pool.wait_ge(s_offs, 1)
            for c in range(C0):
                pool.indirect_dma_start(
                    out=padr[:, c, :, :].rearrange("p e k -> p (e k)"), out_offset=None, in_=rec_d[:, :],
                    in_offset=bass.IndirectOffsetOnAxis(ap=offs[:, c:c + 1], axis=0)).then_inc(s_padr, 16)
            nc.gpsimd.memset(flat[:, ZPOOL:LATE_AT], 0.0)
            pool.wait_ge(s_slots, 1)
            pool.wait_ge(s_sq0, 4)
            nc.gpsimd.memset(flat[:, ZDMA:ZPOOL], 0.0).then_inc(s_zero_pool, 1)

            def gather(k, i=None):
                h = k // HALF
                if k % HALF == 0:
                    pool.wait_ge(s_staged, h + 1 if i is None else i * 2 + (h + 1))
                if i is not None:
                    pool.wait_ge(s_mm, (i - 1) * UN + (k + 1))
                    pool.nop(nofuse=True)
                pool.indirect_dma_start(
                    out=gath[:, k, :], out_offset=None, in_=tab0_d[:, :],
                    in_offset=bass.IndirectOffsetOnAxis(ap=stage[:, h, k % HALF:k % HALF + 1], axis=0),
                ).then_inc(s_gathered[k], 16)

            pool.wait_ge(s_tab0, 16 * (NT - UN + 1))
            for k in range(UN):
                gather(k)
            with pool.Fori(1, SURE) as i:
                for k in range(UN):
                    gather(k, i)
            bodies = bodies_of(pool)
            with pool.Fori(SURE, BODIES) as i:
                with pool.If(bodies > i):
                    for k in range(UN):
                        gather(k, i)

            pool.wait_ge(s_bias, 32)
            for i in range(NT):
                xs = nslot(i, SLOT_X)[0:ROWS[i], :]
                pool.wait_ge(s_xre[i], 16)
                nc.gpsimd.tensor_tensor(xs, xs, hb_t[0:ROWS[i], :], ALU.add).then_inc(s_xb, 1)

        @block.scalar
        def _(act):
            act.wait_ge(s_edges, 96)
            for k, a in enumerate((e_src, e_dst, e_typ, e_wt)):
                nc.scalar.copy(rec[:, :, k], a).then_inc(s_rec, 1)

            for f in range(FT):
                act.wait_ge(s_wtr, f + 1)
                nc.scalar.copy(wt_sb[:, f, :], PS[:, 5 + f % 2, :]).then_inc(s_wev, 1)
            act.wait_ge(s_sq_zero, 1)
            act.wait_ge(s_brow, 16)
            act.wait_ge(s_wc, 64)
            act.wait_ge(s_win, 16)
            for k, a, r in ((SQ_EW, e_wt, EP), (SQ_WC, wc, P), (SQ_W, w_sb.rearrange("p c i -> p (c i)"), P), (SQ_B, b_row, 1)):
                if k:
                    act.wait_ge(s_sq0, k)
                nc.scalar.activation(squares[0:r, 0:a.shape[1]], a, ACT.Square, accum_out=sq[0:r, k:k + 1]).then_inc(s_sq0, 1)
            def rows(t, k):
                bias = neg_col[:, t:t + 1] if isinstance(t, int) else neg_col[:, bass.ds(t, 1)]
                nc.scalar.activation(dist[:, k % 2, :], iota_b[:, :], ACT.Abs, bias=bias, scale=1.0).then_inc(s_dist, 1)
                act.wait_ge(s_dist, t + 1)
                nc.scalar.activation(oh_ad[:, k % 4, :], dist[:, k % 2, :], ACT.Relu, bias=1.0, scale=-1.0).then_inc(s_rows, 1)

            def table_rows():
                act.wait_ge(s_stat0, 1)
                nc.scalar.activation(rstd[:, :], mv[:, :, 1], ACT.Sqrt, bias=eps_t[:, :]).then_inc(s_sd0, 1)
                act.wait_ge(s_nmr0, 1)
                for i in range(NT):
                    r = ROWS[i]
                    nc.scalar.activation(x_tile(i), x_tile(i), ACT.Relu, bias=nmr[0:r, i:i + 1],
                                         scale=rstd[0:r, i:i + 1]).then_inc(s_h0, 1)

            act.wait_ge(s_pev, C0)
            for h in range(2):
                nc.scalar.copy(stage[:, h, :], src0[:, HALF * h:HALF * h + HALF]).then_inc(s_staged, 1)
            act.wait_ge(s_cols, 1)
            for t in range(LEAD):
                rows(t, t)
            for q in range(VG):
                if q == LN_AT:
                    table_rows()
                if q in DIRECT:
                    continue
                act.wait_ge(s_tb, q + 1)
                if q >= 3:
                    act.wait_ge(s_oht, q - 2)
                nc.scalar.copy(types_b[:, q % 3, :], PS[:, q % 4, :]).then_inc(s_types, 1)

            act.wait_ge(s_zero_dma, 16 * 5)

            def copies(i=None, n=None):
                t0 = 0 if i is None else i * UN
                before = 0 if i is None else i * 16
                for k in range(UN):
                    h = k // HALF
                    if k or i is not None:
                        act.wait_ge(s_counted, t0 + k)
                    rows(t0 + (k + LEAD), k + LEAD)
                    if i is not None and k % HALF == 0:
                        act.wait_ge(s_snap_out[h], before)
                    act.wait_ge(s_counted, t0 + (k + 1))
                    nc.scalar.copy(snap[:, h, k % HALF, :], PS[:, 6, 0:CW]).then_inc(s_snap, 1)
                    if k % HALF == 1:
                        for q in range(HALF * h, HALF * h + HALF):
                            act.wait_ge(s_gathered[q], before + 16)
                        nc.scalar.copy(stage[:, h, :], src0[:, bass.ds(t0 + (UN + HALF * h), HALF)]).then_inc(s_staged, 1)
                    if k % HALF == HALF - 1 and n is not None:
                        act.wait_ge(s_piece, (n + h) * 16 + 16)
                        if h or i is not None:
                            act.wait_ge(s_sq, n + h)
                        nc.scalar.activation(piece[:, :], piece[:, :], ACT.Square,
                                             accum_out=sq_piece[:, bass.ds(n + h, 1)]).then_inc(s_sq, 1)

            copies(None, 0)
            with act.Fori(1, PIECES // 2) as i:
                copies(i, i * 2)
            with act.Fori(PIECES // 2, SURE) as i:
                copies(i)
            bodies = bodies_of(act)
            with act.Fori(SURE, BODIES) as i:
                with act.If(bodies > i):
                    copies(i)

            def back(g):
                act.wait_ge(s_zt, g + 1)
                nc.scalar.activation(zparts(g, 0), PS[:, zbank(g), :], ACT.Copy, scale=scale[:, g:g + 1]).then_inc(s_zhi, 1)

            def split(n):
                for h in range(2):
                    act.wait_ge(s_whole[h], 16 * (n + 1))
                    if n < NB:
                        if n >= 2 and h == 0:
                            act.wait_ge(s_base_used, n - 1)
                            act.wait_ge(s_parts_out[n % 2], 16 * (n // 2))
                        there, col = base_ring[:, n % 2, 0, FT // 2 * h:FT // 2 * (h + 1), :], SC_BASE
                    else:
                        there, col = w1t[:, 0, FT // 2 * h:FT // 2 * (h + 1), :], SC_W
                    nc.scalar.activation(there.rearrange("p f o -> p (f o)"), whole[:, h, :], ACT.Copy,
                                         scale=scale[:, col:col + 1]).then_inc(s_whi, 1)

            def keep(p):
                act.wait_ge(s_base_used, NB * (p + 1))
                for c in range(1, FT, 2):
                    for there, here in kept(p, c):
                        last = nc.scalar.activation(there, here, ACT.Copy, scale=unscale[:, SC_BASE:SC_BASE + 1])
                    last.then_inc(s_accfree[1], 1)

            def turned_h(i):
                r = ROWS[i]
                act.wait_ge(s_htr, i + 1)
                nc.scalar.copy(parts(i, SLOT_HT, 0).rearrange("p (f n) -> p f n", f=FT)[:, :, 0:r],
                               PS[:, 6, :].rearrange("p (f n) -> p f n", f=FT)[:, :, 0:r]).then_inc(s_hhi, 1)

            def scaled_u(i):
                r = ROWS[i]
                act.wait_ge(s_ub, i + 1)
                nc.scalar.activation(parts(i, SLOT_U, 0)[0:r, :], nslot(i, SLOT_H)[0:r, :], ACT.Copy,
                                     scale=dis_up[0:r, i:i + 1]).then_inc(s_uhi, 1)

            def normalise(i):
                r = ROWS[i]
                act.wait_ge(s_stat1, i + 1)
                nc.scalar.activation(rstd[0:r, i:i + 1], mv[0:r, i, 1:2], ACT.Sqrt, bias=eps_t[0:r, :]).then_inc(s_sd1, 1)
                act.wait_ge(s_nmr1, i + 1)
                nc.scalar.activation(nslot(i, SLOT_H)[0:r, :], nslot(i, SLOT_X1)[0:r, :], ACT.Relu,
                                     bias=nmr[0:r, i:i + 1], scale=rstd[0:r, i:i + 1]).then_inc(s_h1, 1)

            act.wait_ge(s_scale[0], 1)
            for g in range(FIRST):
                if g == FIRST // 2:
                    act.wait_ge(s_scale[1], 1)
                    split(0)
                back(g)
            for p in range(len(PASSES)):
                if p:
                    keep(p - 1)
                for b in range(NB):
                    groups = later_groups(p, b)
                    for g in groups[:2]:
                        back(g)
                    if p == 0 and b + 1 < NB:
                        split(b + 1)
                    for g in groups[2:]:
                        back(g)
                    if p == 1 and b == 0:
                        split(NB)
                    if (p, b) == (0, 0):
                        act.wait_ge(s_deg, 1)
                        nc.scalar.activation(dis[:, :], dis[:, :], ACT.Sqrt).then_inc(s_deg_sqrt, 1)
                    if prev_tile(p, b - 1) is not None:
                        turned_h(prev_tile(p, b - 1))
                    if prev_tile(p, b - 2) is not None:
                        scaled_u(prev_tile(p, b - 2))
                    if prev_tile(p, b) is not None:
                        normalise(prev_tile(p, b))
            keep(len(PASSES) - 1)
            for i in PASSES[-1]:
                normalise(i)
                turned_h(i)
                scaled_u(i)
            for i in range(NT):
                r = ROWS[i]
                act.wait_ge(s_fin, i + 1)
                if i >= UN:
                    act.wait_ge(s_res, i - UN + 1)
                nc.scalar.activation(gath[0:r, i % UN, :], PS[0:r, FBANK[i], :], ACT.Relu,
                                     scale=dis[0:r, i:i + 1]).then_inc(s_relu, 1)

        @block.vector
        def _(dve):
            v = nc.vector
            chain = [0]

            def link(ins):
                ins.then_inc(s_link, 1)
                chain[0] += 1
                dve.wait_ge(s_link, chain[0])

            v.memset(e_nxt, 1 << 20).then_inc(s_fill, 1)
            v.memset(ones[:, :], 1.0)
            v.memset(eps_t[:, :], EPS)
            v.memset(snap[:, :, :, :], 0).then_inc(s_zero_src, 1)
            v.memset(mv[:, :, :], 0.0)
            v.memset(sq[:, :], 0.0).then_inc(s_sq_zero, 1)
            v.memset(big_t[:, :], 0)
            dve.wait_ge(s_iota, 3)
            v.tensor_copy(iota_f[:, :], iota_i[:, 0:P])
            v.tensor_copy(iota_b[:, :], iota_i)
            link(v.tensor_copy(part_f[:, :], part_i[:, :]))
            v.tensor_scalar(ident[:, :], iota_f[:, :], part_f[:, :], None, ALU.is_equal).then_inc(s_ident, 1)
            v.tensor_copy(iota_ps, iota_f[:, 0:GD])
            v.tensor_scalar(pm_i[:, 0:1], part_i[:, :], TG - 1, None, ALU.bitwise_and)
            link(v.tensor_scalar(pm_i[:, 1:2], part_i[:, :], 3, None, ALU.logical_shift_right))
            link(v.tensor_copy(pm_f[:, 0:2], pm_i[:, 0:2]))
            v.tensor_scalar(m_j, iota_f[:, 0:TG], pm_f[:, 0:1], None, ALU.is_equal)
            link(v.tensor_scalar(m_a, iota_f[:, 0:NT], pm_f[:, 1:2], None, ALU.is_equal))

            link(v.tensor_scalar(pm_i[:, 2:3], part_i[:, :], 4, None, ALU.logical_shift_right))
            link(v.tensor_copy(pm_f[:, 2:3], pm_i[:, 2:3]))
            v.tensor_scalar(m_g[:, :], iota_f[:, 0:TG], pm_f[:, 2:3], None, ALU.is_equal)
            dve.wait_ge(s_edges, 96)
            link(v.tensor_scalar(t_i, e_dst, 7, None, ALU.logical_shift_right))
            link(v.tensor_copy(ga, t_i))
            link(v.tensor_scalar(t_i, e_dst, 4, TG - 1, ALU.logical_shift_right, ALU.bitwise_and))
            link(v.tensor_copy(gb, t_i))
            for a in range(NT):
                v.tensor_scalar(oh_ga[:, a, :], ga, float(a), None, ALU.is_equal).then_inc(s_ohg, 1)
            for b in range(TG):
                v.tensor_scalar(oh_gb[:, b, :], gb, float(b), None, ALU.is_equal).then_inc(s_ohg, 1)
            link(v.tensor_tensor(viol, e_dst, e_nxt, ALU.is_gt))
            link(v.reduce_sum(viol_s, viol, AX.X))

            K = NT * TG
            dve.wait_ge(s_cnt_part, 1)
            link(v.tensor_tensor(tmp_g[0:K], PS[0:K, 0, 0:TG * TG].rearrange("p (b j) -> p b j", j=TG),
                                 m_j[0:K, :].unsqueeze(1).to_broadcast([K, TG, TG]), ALU.mult))
            link(v.reduce_sum(prt_g[0:K, :], tmp_g[0:K], AX.X))
            v.tensor_tensor(exp_g[0:K, :].rearrange("p (a b) -> p a b", a=NT),
                            prt_g[0:K, :].unsqueeze(1).to_broadcast([K, NT, TG]),
                            m_a[0:K, :].unsqueeze(2).to_broadcast([K, NT, TG]), ALU.mult).then_inc(s_exp, 1)

            dve.wait_ge(s_cnt, 1)
            v.tensor_scalar(flag[0:1, :], PS[0:1, 1, NGP:NGP + 1], 1.0, None, ALU.min).then_inc(s_flag, 1)
            link(v.tensor_copy(cnt, PS[:, 1, 0:NGP]))
            v.tensor_tensor(bound[:, 0:NGP], cnt, cnt, ALU.mult)

            def chunks(cnt_, nch_, nch_i_, kend_, dD_, n):
                link(v.tensor_scalar(nch_i_, cnt_, float(P - 1), None, ALU.add))
                link(v.tensor_scalar(nch_i_, nch_i_, 7, None, ALU.logical_shift_right))
                link(v.tensor_copy(nch_, nch_i_))
                v.scalar_tensor_tensor(dD_, nch_, -float(P), cnt_, ALU.mult, ALU.add)
                link(v.tensor_tensor_scan(kend_, ones[:, 0:n], nch_, 0.0, ALU.mult, ALU.add))

            chunks(cnt, nch, nch_i, kend, dD, NGP)
            link(v.tensor_tensor_scan(cum, ones[:, 0:NGP], cnt, 0.0, ALU.mult, ALU.add))
            link(v.tensor_scalar(bodies_t[0:1, :], kend[0:1, NG - 1:NG], float(UN - 1), None, ALU.add))
            v.tensor_scalar(bodies_t[0:1, :], bodies_t[0:1, :], UN.bit_length() - 1, None,
                            ALU.logical_shift_right).then_inc(s_bodies, 1)
            v.memset(ends[0:1, 0:1], 0)
            v.tensor_copy(ends[0:1, 1:NGP + 1], kend[0:1, :])
            for c in range(C0):
                last = v.tensor_scalar(tt[:, c:c + 1], part_f[:, :], float(P * c), None, ALU.add)
            link(last)
            link(v.tensor_tensor(le, kend.unsqueeze(1).to_broadcast([P, C0, NGP]),
                                 tt.unsqueeze(2).to_broadcast([P, C0, NGP]), ALU.is_le))
            v.reduce_sum(gt, le, AX.X)
            link(v.tensor_tensor(junk, le, dD.unsqueeze(1).to_broadcast([P, C0, NGP]), ALU.mult))
            link(v.reduce_sum(oacc, junk, AX.X))
            link(v.scalar_tensor_tensor(oacc, tt, float(P), oacc, ALU.mult, ALU.add))
            v.tensor_scalar(offs, oacc, float(E), None, ALU.min).then_inc(s_offs, 1)
            link(v.tensor_scalar(gt, gt, float(NG - 1), None, ALU.min))
            v.tensor_scalar(gsc, gt, float(GD), None, ALU.mult)
            v.tensor_tensor(so_next[0:1, :], cum[0:1, :], cnt[0:1, :], ALU.subtract).then_inc(s_table, 1)

            dve.wait_ge(s_flag, 1)
            unsorted = dve.value_load(flag[0:1, 0:1], min_val=0, max_val=1)
            with dve.If(unsorted > 0):
                v.tensor_scalar(tri, iota_f[:, :], part_f[:, :], None, ALU.is_gt)
                dve.wait_ge(s_rec, 5)
                with dve.Fori(0, EC) as j:
                    dve.wait_ge(s_so_out, j * 16)
                    v.tensor_copy(so_rec, rec[:, bass.ds(j, 1), :].rearrange("p c k -> p (c k)")).then_inc(s_so_v, 1)
                    dve.wait_ge(s_so_v, j * 7 + 1)
                    v.tensor_copy(so_dst, so_rec[:, 1:2]).then_inc(s_so_v, 1)
                    dve.wait_ge(s_so_v, j * 7 + 2)
                    v.tensor_scalar(so_dst, so_dst, 4, None, ALU.logical_shift_right).then_inc(s_so_v, 1)
                    dve.wait_ge(s_so_v, j * 7 + 3)
                    v.tensor_copy(so_grp, so_dst).then_inc(s_so_v, 1)
                    dve.wait_ge(s_so_v, j * 7 + 4)
                    v.tensor_scalar(so_oh, iota_f[0:EP, 0:NGP], so_grp, None, ALU.is_equal).then_inc(s_so_oh, 1)
                    dve.wait_ge(s_so_mm, j + 1)
                    v.tensor_tensor(so_prod, PS[0:EP, 2, 0:NGP], so_oh, ALU.mult).then_inc(s_so_v, 1)
                    v.tensor_tensor(so_next[0:1, :], PS[0:1, 3, 0:NGP], so_next[0:1, :], ALU.add).then_inc(s_so_v, 1)
                    dve.wait_ge(s_so_v, j * 7 + 6)
                    v.reduce_sum(so_posf, so_prod, AX.X).then_inc(s_so_v, 1)
                    dve.wait_ge(s_so_v, j * 7 + 7)
                    v.tensor_copy(so_pos, so_posf).then_inc(s_so_pos, 1)

            def moments0(i):
                r = ROWS[i]
                link(v.bn_stats(stats[0:r, :], x_tile(i)))
                link(v.bn_aggr(mv[0:r, i, :], stats[0:r, :]))
                if i == NT - 1:
                    v.memset(stats[:, :], 0.0).then_inc(s_stat0, 1)

            dve.wait_ge(s_wc, 64)
            link(v.tensor_scalar(blk_i, part_i[:, :], 5, None, ALU.logical_shift_right))
            link(v.tensor_copy(blk, blk_i))
            link(v.scalar_tensor_tensor(rel, blk, -float(R), part_f[:, :], ALU.mult, ALU.add))
            link(v.tensor_scalar(wbm, iota_f[:, 0:4], blk, None, ALU.is_equal))
            link(v.tensor_tensor(wblk, wc.unsqueeze(1).to_broadcast([P, 4, NB]),
                                 wbm.unsqueeze(2).to_broadcast([P, 4, NB]), ALU.mult))
            for s in range(3):
                part = wparts[:, s, :].rearrange("p (t b) -> p t b", b=NB)
                if s < 2:
                    link(v.tensor_copy(part, wblk))
                    link(v.tensor_tensor(wblk, wblk, part, ALU.subtract))
                else:
                    v.tensor_copy(part, wblk).then_inc(s_wparts, 1)

            dve.wait_ge(s_slot_ps, 1)
            v.tensor_copy(slots[0:1, :], PS[0:1, 4, 0:T0P]).then_inc(s_slots, 1)
            dve.wait_ge(s_xin, 16 * (NT - UN + 1))
            for i in range(XEARLY):
                moments0(i)
            dve.wait_ge(s_padr, 16 * C0)
            for c in range(C0):
                v.tensor_scalar(padr[:, c, :, 1], padr[:, c, :, 1], gsc[:, c:c + 1], None, ALU.subtract).then_inc(s_ploc, 1)
            for c in range(C0):
                v.tensor_copy(typ16[:, c, :], padr[:, c, :, 2]).then_inc(s_ploc, 1)
            for c in range(C0):
                bank = 2 + c % 2
                dve.wait_ge(s_ptr, c + 1)
                n = min(P, T0P - P * c)
                v.tensor_copy(dloc0[:, P * c:P * c + n], PS[:, bank, 0:n])
                v.tensor_copy(wtT[:, P * c:P * c + P], PS[:, bank, 2 * P:3 * P])
                v.tensor_copy(src0[:, P * c:P * c + n], PS[:, bank, P:P + n]).then_inc(s_pev, 1)
            dve.wait_ge(s_pev, C0)
            link(v.tensor_scalar(part_of, src0, P - 1, None, ALU.bitwise_and))
            link(v.tensor_copy(src_in, part_of))
            link(v.tensor_scalar(part_of, src0, 7, None, ALU.logical_shift_right))
            link(v.tensor_copy(tile_of, part_of))
            link(v.tensor_scalar(outside, dloc0, GD - 0.5, 1024.0, ALU.is_gt, ALU.mult))
            link(v.scalar_tensor_tensor(neg_col, tile_of, -float(GD), dloc0, ALU.mult, ALU.subtract))
            v.tensor_tensor(neg_col, neg_col, outside, ALU.subtract).then_inc(s_cols, 1)
            dve.wait_ge(s_cols, 1)

            def largest(n):
                dve.wait_ge(s_sqt[n], 1)
                link(v.tensor_reduce(sq_max[0:NSQ, :], PS[0:NSQ, 4, 0:P], AX.X, ALU.max))
                v.tensor_scalar(sq_diag[0:NSQ, :], ident[0:NSQ, 0:NSQ], sq_max[0:NSQ, :], None, ALU.mult).then_inc(s_sqd[n], 1)
                dve.wait_ge(s_sqall[n], 1)
                link(v.tensor_copy(sq_all[:, :], PS[:, 5, 0:NSQ]))

            def powers(a, b):
                bd, he, sc, us = (t[:, a:b] for t in (bound, half_e, scale_i, unscale_i))
                link(v.tensor_scalar(bd, bd, 1e-36, 1e36, ALU.max, ALU.min))
                link(v.tensor_scalar(he, bd.bitcast(i32), 23, None, ALU.logical_shift_right))
                link(v.tensor_scalar(he, he, 3.0, None, ALU.add))
                link(v.tensor_scalar(he, he, 1, None, ALU.logical_shift_right))
                v.tensor_scalar(sc, he, -1.0, 127.0 + 79.0, ALU.mult, ALU.add)
                link(v.tensor_scalar(us, he, 127.0 - 79.0, None, ALU.add))
                v.tensor_scalar(sc, sc, 23, None, ALU.logical_shift_left)
                link(v.tensor_scalar(us, us, 23, None, ALU.logical_shift_left))

            HH = 1.001 * D
            largest(0)
            link(v.tensor_scalar(sq_max[:, :], sq_all[:, SQ_EW:SQ_EW + 1], sq_all[:, SQ_WC:SQ_WC + 1], HH, ALU.mult, ALU.mult))
            link(v.tensor_scalar(bound[:, 0:NGP], bound[:, 0:NGP], sq_max[:, :], None, ALU.mult))
            powers(0, NGP)
            link(v.tensor_tensor(unscale_g[:, :].rearrange("p (i j) -> p i j", j=TG),
                                 unscale[:, 0:NGP].rearrange("p (i j) -> p i j", j=TG),
                                 m_g[:, :].unsqueeze(1).to_broadcast([P, NT, TG]), ALU.mult))
            v.reduce_sum(unscale_n[:, :], unscale_g[:, :].rearrange("p (i j) -> p i j", j=TG), AX.X).then_inc(s_scale[0], 1)
            def value(q):
                dve.wait_ge(s_look, q + 1)
                v.tensor_tensor(val_v[:, 16 * q:16 * q + 16, :],
                                PS[:, 4 + q % 2, 0:16 * NB].rearrange("p (t b) -> p t b", b=NB),
                                wtT[:, 16 * q:16 * q + 16].unsqueeze(2).to_broadcast([P, 16, NB]),
                                ALU.mult).then_inc(s_val, 1)

            for q in range(VG):
                if q == LN_AT:
                    dve.wait_ge(s_sd0, 1)
                    link(v.reciprocal(rstd[:, :], rstd[:, :]))
                    v.scalar_tensor_tensor(nmr[:, :], mv[:, :, 0], -1.0, rstd[:, :], ALU.mult, ALU.mult).then_inc(s_nmr0, 1)
                if q in DIRECT:
                    dve.wait_ge(s_tb, q + 1)
                    there = PS[:, q % 4, :]
                else:
                    dve.wait_ge(s_types, len([k for k in range(q + 1) if k not in DIRECT]))
                    there = types_b[:, q % 3, :]
                if q >= 2:
                    dve.wait_ge(s_look, q - 1)
                v.tensor_scalar(oh_t[:, q % 2, :], there, rel, None, ALU.is_equal).then_inc(s_oht, 1)
                if q + XEARLY < NT:
                    moments0(q + XEARLY)
                if q >= 1:
                    value(q - 1)
            value(VG - 1)
            def col(tab, t):
                return tab[:, t:t + 1] if isinstance(t, int) else tab[:, bass.ds(t, 1)]

            def select(k, t):
                v.tensor_scalar(oh_r[:, k % 4, :], iota_b[:, 0:P], col(src_in, t), None, ALU.is_equal)
                vals = val[:, t * NB:t * NB + NB] if isinstance(t, int) else val[:, bass.ds(t * NB, NB)]
                v.scalar_tensor_tensor(
                    sel[:, k % 4, :].rearrange("p (b d) -> p b d", b=NB), iota_ps.unsqueeze(1).to_broadcast([P, NB, GD]),
                    col(dloc0, t), vals.unsqueeze(2).to_broadcast([P, NB, GD]), ALU.is_equal, ALU.mult
                    ).then_inc(s_selected, 1)

            for t in range(LEAD):
                select(t, t)

            dve.wait_ge(s_val, VG)
            v.memset(flat[:, LOOK_AT:MID_AT], 0.0)

            dve.wait_ge(s_zero_dma, 16 * 5)
            dve.wait_ge(s_zero_pool, 1)

            def sums(i=None):
                t0 = 0 if i is None else i * UN
                for k in range(UN):
                    if k or i is not None:
                        dve.wait_ge(s_counted, t0 + k)
                    select(k + LEAD, t0 + (k + LEAD))
                    if k == 0:
                        row = nc.values_load_multi_w_load_instructions(
                            slots[0:1, bass.ds(t0, UN)], engines=bass.OrderedEngineSet([dve.engine]),
                            min_val=0, max_val=NG - 1,
                            skip_runtime_bounds_check_because="the table's values are clamped to the last slot")[1]
                    dve.wait_ge(s_mm, t0 + (k + 1))
                    if k or i is not None:
                        dve.wait_ge(s_added, t0 + k)
                    z = Z[:, bass.ds(row[k], 1), :].rearrange("p a d -> p (a d)")
                    v.tensor_tensor(z, z, PS[:, k % NPB, :], ALU.add).then_inc(s_added, 1)

            sums()
            with dve.Fori(1, SURE) as i:
                sums(i)
            bodies = bodies_of(dve)
            with dve.Fori(SURE, BODIES) as i:
                with dve.If(bodies > i):
                    sums(i)

            def matrices():
                v.tensor_reduce(sq[:, SQ_BASE:SQ_BASE + 1], sq_piece[:, :], AX.X, ALU.max).then_inc(s_base_sq, 1)
                largest(1)
                v.tensor_copy(bound[:, SC_BASE:SC_BASE + 1], sq_all[:, SQ_BASE:SQ_BASE + 1])
                v.tensor_copy(bound[:, SC_W:SC_W + 1], sq_all[:, SQ_W:SQ_W + 1])
                link(v.scalar_tensor_tensor(bound[:, SC_U:SC_U + 1], sq_all[:, SQ_W:SQ_W + 1], HH, sq_all[:, SQ_B:SQ_B + 1],
                                            ALU.mult, ALU.add))
                link(v.tensor_scalar(bound[:, SC_U:SC_U + 1], bound[:, SC_U:SC_U + 1], 2.0, None, ALU.mult))
                powers(NGP, NSC)
                v.memset(sq_max[:, :], 0.0).then_inc(s_scale[1], 1)

            def degrees():
                dve.wait_ge(s_scale[1], 1)
                dve.wait_ge(s_snap, bodies * UN)
                link(v.tensor_reduce(sq_max[:, :], PS[:, 6, 0:CW], AX.X, ALU.max))
                link(v.reduce_sum(dis[:, :], PS[:, 6, 0:CW].rearrange("p (a d) -> p a d", a=NT), AX.X))
                v.tensor_scalar(dis[:, :], dis[:, :], 1.0, None, ALU.add).then_inc(s_deg, 1)

            def node_scales():
                dve.wait_ge(s_deg_sqrt, 1)
                link(v.reciprocal(dis[:, :], dis[:, :]))
                link(v.tensor_scalar(dis_up[:, :], dis[:, :], scale[:, SC_U:SC_U + 1], None, ALU.mult))
                v.tensor_scalar(dis[:, :], dis[:, :], unscale[:, SC_U:SC_U + 1], None, ALU.mult).then_inc(s_dis, 1)

            def any_big():
                dve.wait_ge(s_big_t, 1)
                link(v.tensor_reduce(sq_diag[0:1, 0:1], PS[0:1, 7, 0:P], AX.X, ALU.max))
                v.tensor_scalar(big_t[:, :], sq_diag[0:1, 0:1], 2047.5, None, ALU.is_gt).then_inc(s_big, 1)
                dve.wait_ge(s_big, 1)
                big = dve.value_load(big_t[0:1, 0:1], min_val=0, max_val=1)
                return big

            def back(g):
                dve.wait_ge(s_zhi, g + 1)
                v.scalar_tensor_tensor(zparts(g, 1), PS[:, zbank(g), :], scale[:, g:g + 1], zparts(g, 0),
                                       ALU.mult, ALU.subtract).then_inc(s_zlo, 1)

            def split(n):
                ring, col = (base_ring[:, n % 2], SC_BASE) if n < NB else (w1t, SC_W)
                for h in range(2):
                    dve.wait_ge(s_whi, 2 * n + h + 1)
                    hi, lo = (ring[:, s, FT // 2 * h:FT // 2 * (h + 1), :].rearrange("p f o -> p (f o)") for s in range(2))
                    v.scalar_tensor_tensor(lo, whole[:, h, :], scale[:, col:col + 1], hi, ALU.mult, ALU.subtract
                                           ).then_inc(s_wlo, 1)

            def keep(p):
                dve.wait_ge(s_base_used, NB * (p + 1))
                for c in range(0, FT, 2):
                    for there, here in kept(p, c):
                        last = v.tensor_scalar(there, here, unscale[:, SC_BASE:SC_BASE + 1], None, ALU.mult)
                    last.then_inc(s_accfree[0], 1)

            def moments(i):
                r = ROWS[i]
                x1 = nslot(i, SLOT_X1)[0:r, :]
                dve.wait_ge(s_xb, i + 1)
                dve.wait_ge(s_xtr, i + 1)
                v.scalar_tensor_tensor(x1, PS[0:r, 6, :], unscale_n[0:r, i:i + 1], nslot(i, SLOT_X)[0:r, :],
                                       ALU.mult, ALU.add).then_inc(s_x1, 1)
                dve.wait_ge(s_x1, i + 1)
                v.bn_stats(stats[0:r, :], x1).then_inc(s_bn, 1)
                dve.wait_ge(s_bn, i + 1)
                v.bn_aggr(mv[0:r, i, :], stats[0:r, :]).then_inc(s_stat1, 1)
                dve.wait_ge(s_sd1, i + 1)
                v.reciprocal(rstd[0:r, i:i + 1], rstd[0:r, i:i + 1]).then_inc(s_rcp1, 1)
                dve.wait_ge(s_rcp1, i + 1)
                v.scalar_tensor_tensor(nmr[0:r, i:i + 1], mv[0:r, i, 0:1], -1.0, rstd[0:r, i:i + 1],
                                       ALU.mult, ALU.mult).then_inc(s_nmr1, 1)

            def turned_h(i):
                r = ROWS[i]
                hi, lo = (parts(i, SLOT_HT, s).rearrange("p (f n) -> p f n", f=FT)[:, :, 0:r] for s in range(2))
                dve.wait_ge(s_hhi, i + 1)
                v.tensor_tensor(lo, PS[:, 6, :].rearrange("p (f n) -> p f n", f=FT)[:, :, 0:r], hi,
                                ALU.subtract).then_inc(s_hlo, 1)

            def add_b(i):
                r = ROWS[i]
                dve.wait_ge(s_u, i + 1)
                v.scalar_tensor_tensor(nslot(i, SLOT_H)[0:r, :], PS[0:r, 7, :], unscale[0:r, SC_W:SC_W + 1], b1_t[0:r, :],
                                       ALU.mult, ALU.add).then_inc(s_ub, 1)

            def scale_u(i):
                r = ROWS[i]
                dve.wait_ge(s_uhi, i + 1)
                v.scalar_tensor_tensor(parts(i, SLOT_U, 1)[0:r, :], nslot(i, SLOT_H)[0:r, :], dis_up[0:r, i:i + 1],
                                       parts(i, SLOT_U, 0)[0:r, :], ALU.mult, ALU.subtract).then_inc(s_uev, 1)

            def counts(j):
                n = len(GROUPS[j])
                dve.wait_ge(s_raw[j % 2], raw_done(j))

                def gain(there):
                    return v.tensor_tensor(there[:, :, 0:GD * n].rearrange("p a (g d) -> p g a d", g=n),
                                           raw[:, j % 2, 1:n + 1, :].rearrange("p g (a d) -> p g a d", a=NT),
                                           raw[:, j % 2, 0:n, :].rearrange("p g (a d) -> p g a d", a=NT),
                                           ALU.subtract)

                def own(s):
                    there = counts_of(j, s)[:, j, 0:GD * n]
                    v.tensor_tensor(there, there, ident[:, 0:GD * n], ALU.add).then_inc(s_counts, 1)

                gain(counts_of(j)).then_inc(s_split, 1)
                with dve.If(big > 0):
                    gain(gained).then_inc(s_diff, 1)
                    dve.wait_ge(s_split, j + 1)
                    dve.wait_ge(s_diff, j + 1)
                    v.tensor_tensor(counts_of(j, 1)[:, :, 0:GD * n], gained[:, :, 0:GD * n], counts_of(j)[:, :, 0:GD * n],
                                    ALU.subtract).then_inc(s_rest, 1)
                    dve.wait_ge(s_rest, j + 1)
                    own(1)
                with dve.Else():
                    dve.wait_ge(s_split, j + 1)
                    own(0)

            for g in range(FIRST):
                if g == FIRST // 2:
                    matrices()
                    split(0)
                back(g)
            for p in range(len(PASSES)):
                if p:
                    keep(p - 1)
                for b in range(NB):
                    groups = later_groups(p, b)
                    for g in groups[:2]:
                        back(g)
                    if p == 0 and b + 1 < NB:
                        split(b + 1)
                    for g in groups[2:]:
                        back(g)
                    if p == 1 and b == 0:
                        split(NB)
                    if (p, b) == (0, 0):
                        degrees()
                    if (p, b) == (0, 1):
                        node_scales()
                        big = any_big()
                    if counts_step(p, b) is not None:
                        counts(counts_step(p, b))
                    if prev_tile(p, b - 1) is not None:
                        turned_h(prev_tile(p, b - 1))
                    if prev_tile(p, b - 2) is not None:
                        add_b(prev_tile(p, b - 2))
                        scale_u(prev_tile(p, b - 2))
                    if prev_tile(p, b) is not None:
                        moments(prev_tile(p, b))
            keep(len(PASSES) - 1)
            for i in PASSES[-1]:
                moments(i)
                turned_h(i)
                add_b(i)
                scale_u(i)
            for i in range(NT):
                r = ROWS[i]
                x1 = nslot(i, SLOT_X1)[0:r, :]
                dve.wait_ge(s_relu, i + 1)
                v.tensor_tensor(x1, gath[0:r, i % UN, :], x1, ALU.add).then_inc(s_res, 1)

        @block.tensor
        def _(pe):
            mm, tr = nc.tensor.matmul, nc.tensor.transpose
            pe.wait_ge(s_ohg, NT + TG)
            K = NT * TG
            for j in range(EC // TG):
                st = EC // TG
                last = mm(PS[0:K, 0, 0:TG * TG], flat_ga[:, j::st], flat_gb[:, j::st], start=(j == 0), stop=(j == st - 1))
            last.then_inc(s_cnt_part, 1)
            pe.wait_ge(s_exp, 1)
            mm(PS[:, 1, 0:NGP], ones[0:K, :], exp_g[0:K, :], start=True, stop=True)
            mm(PS[:, 1, NGP:NGP + 1], ones[0:EP, :], viol_s, start=True, stop=True).then_inc(s_cnt, 1)

            pe.wait_ge(s_win, 16)
            pe.wait_ge(s_ident, 1)
            for f in range(FT):
                if f >= 2:
                    pe.wait_ge(s_wev, f - 1)
                for c in range(FT):
                    last = tr(PS[:, 5 + f % 2, P * c:P * (c + 1)], w_sb[:, c, P * f:P * (f + 1)], ident[:, :])
                last.then_inc(s_wtr, 1)

            pe.wait_ge(s_flag, 1)
            unsorted = pe.value_load(flag[0:1, 0:1], min_val=0, max_val=1)
            with pe.If(unsorted > 0):
                with pe.Fori(0, EC) as j:
                    pe.wait_ge(s_so_oh, j + 1)
                    mm(PS[0:EP, 2, 0:NGP], tri[0:EP, 0:EP], so_oh, start=True, stop=False)
                    mm(PS[0:EP, 2, 0:NGP], ones[0:1, 0:EP], so_next[0:1, :], start=False, stop=True)
                    mm(PS[0:1, 3, 0:NGP], ones[0:EP, 0:1], so_oh, start=True, stop=True).then_inc(s_so_mm, 1)

            pe.wait_ge(s_table, 1)
            for c in range(C0):
                last = mm(PS[0:1, 4, P * c:P * (c + 1)], gt[:, c:c + 1], ident[:, :], start=True, stop=True)
            last.then_inc(s_slot_ps, 1)

            pe.wait_ge(s_slots, 1)
            pe.wait_ge(s_ploc, 2 * C0)
            for c in range(C0):
                if c >= 2:
                    pe.wait_ge(s_pev, c - 1)
                for at, field in enumerate((1, 0, 3)):
                    last = tr(PS[:, 2 + c % 2, P * at:P * (at + 1)], padr[:, c, :, field], ident[:, :])
                last.then_inc(s_ptr, 1)
            pe.wait_ge(s_pev, C0)
            pe.wait_ge(s_expand, 1)
            pe.wait_ge(s_wparts, 1)

            def largest(n):
                tr(PS[0:NSQ, 4, 0:P], sq[:, :], ident[:, :]).then_inc(s_sqt[n], 1)
                pe.wait_ge(s_sqd[n], 1)
                mm(PS[:, 5, 0:NSQ], ones[0:NSQ, :], sq_diag[0:NSQ, :], start=True, stop=True).then_inc(s_sqall[n], 1)

            pe.wait_ge(s_sq0, 4)
            largest(0)
            def types(q):
                if q >= 4:
                    pe.wait_ge(s_oht, q - 3)
                for j in range(4):
                    t = (16 * q + 4 * j) % P
                    last = mm(PS[:, q % 4, P * j:P * (j + 1)], expand[:, t:t + 4, :], typ16[:, 16 * q // P, :],
                              start=True, stop=True)
                last.then_inc(s_tb, 1)

            def lookup(q):
                pe.wait_ge(s_oht, q + 1)
                if q >= 2:
                    pe.wait_ge(s_val, q - 1)
                for j in range(4):
                    for s in range(3):
                        last = mm(PS[:, 4 + q % 2, 4 * NB * j:4 * NB * (j + 1)], oh_t[:, q % 2, P * j:P * (j + 1)],
                                  wparts[:, s, :], start=(s == 0), stop=(s == 2))
                last.then_inc(s_look, 1)

            types(0)
            types(1)
            for q in range(VG):
                if q + 2 < VG:
                    types(q + 2)
                lookup(q)

            def chunk(k, i=None):
                if i is None:
                    pe.wait_ge(s_gathered[k], 16)
                    pe.wait_ge(s_selected, k + 1)
                    if k >= NPB:
                        pe.wait_ge(s_added, k - NPB + 1)
                else:
                    pe.wait_ge(s_gathered[k], i * 16 + 16)
                    pe.wait_ge(s_selected, i * UN + (k + 1))
                    pe.wait_ge(s_added, (i - 1) * UN + (k + 1 + UN - NPB))
                mm(PS[:, k % NPB, :], sel[:, k % 4, :], gath[:, k, :], start=True, stop=True).then_inc(s_mm, 1)
                first = i is None and k == 0
                if i is None:
                    pe.wait_ge(s_rows, k + 1)
                    if k:
                        pe.wait_ge(s_snap, k)
                else:
                    pe.wait_ge(s_rows, i * UN + (k + 1))
                    pe.wait_ge(s_snap, i * UN + k)
                mm(PS[:, 6, 0:CW], oh_r[:, k % 4, :], oh_ad[:, k % 4, :], start=first, stop=True,
                   skip_group_check=not first).then_inc(s_counted, 1)

            pe.wait_ge(s_val, VG)
            for k in range(UN):
                chunk(k)
            with pe.Fori(1, SURE) as i:
                for k in range(UN):
                    chunk(k, i)
            bodies = bodies_of(pe)
            with pe.Fori(SURE, BODIES) as i:
                with pe.If(bodies > i):
                    for k in range(UN):
                        chunk(k, i)

            def turn(g):
                if zbank_before(g):
                    pe.wait_ge(s_zlo, zbank_before(g))
                for f in range(FT):
                    last = tr(PS[:, zbank(g), P * f:P * (f + 1)], Z[:, g, P * f:P * (f + 1)], ident[:, :])
                last.then_inc(s_zt, 1)

            def turn_x(i):
                r = ROWS[i]
                if i == PASSES[-1][0]:
                    pe.wait_ge(s_accfree[0], 2 * len(PASSES))
                    pe.wait_ge(s_accfree[1], 2 * len(PASSES))
                if i:
                    pe.wait_ge(s_hlo, i)
                for f in range(FT):
                    last = tr(PS[0:r, 6, P * f:P * (f + 1)], nslot(i, SLOT_XT)[:, P * f:P * f + r], ident[:, :])
                last.then_inc(s_xtr, 1)

            def turn_h(i):
                r = ROWS[i]
                pe.wait_ge(s_h1, i + 1)
                for f in range(FT):
                    last = tr(PS[:, 6, P * f:P * f + r], nslot(i, SLOT_H)[0:r, P * f:P * (f + 1)], ident[0:r, 0:r])
                last.then_inc(s_htr, 1)

            def project(i):
                r = ROWS[i]
                pe.wait_ge(s_hlo, i + 1)
                if i:
                    pe.wait_ge(s_ub, i)
                else:
                    pe.wait_ge(s_wlo, 2 * NB + 2)
                for f in range(FT):
                    for s, q in ((0, 0), (0, 1), (1, 0)):
                        last = mm(PS[0:r, 7, :], parts(i, SLOT_HT, s)[:, P * f:P * f + r], w1t[:, q, f, :],
                                  start=(f == s == q == 0), stop=(f == FT - 1 and s == 1))
                last.then_inc(s_u, 1)

            pe.wait_ge(s_added, bodies * UN)
            for g in range(FIRST):
                if g == FIRST // 2:
                    pe.wait_ge(s_base_sq, 1)
                    largest(1)
                turn(g)
            n = 0
            for p, tiles in enumerate(PASSES):
                pe.wait_ge(s_zlo, GROUPS[tiles[-1]][-1] + 1)
                gs = [g for i in tiles for g in GROUPS[i]]
                nodes = GD * len(gs)
                for b in range(NB):
                    if p == 0:
                        pe.wait_ge(s_wlo, 2 * b + 2)
                    else:
                        pe.wait_ge(s_base[n % 2], 16 * ((n - NB) // 2 + 1))
                    for c in range(FT):
                        if p and b == 0:
                            pe.wait_ge(s_accfree[c % 2], 2 * (p - 1) + c // 2 + 1)
                        for f in range(FT):
                            at = P * f + GD * b
                            for s, q in ((0, 0), (0, 1), (1, 0)):
                                zs = Z[:, gs[0]:gs[-1] + 1, :].rearrange("p g d -> p (g d)").bitcast(f16).rearrange(
                                    "p (g n) -> p g n", n=2 * D)[:, :, D * q + at:D * q + at + GD]
                                last = mm(PS[:, c, 0:nodes], base_ring[:, n % 2, s, f, P * c:P * (c + 1)], zs,
                                          start=(b == f == s == q == 0), stop=(b == NB - 1 and f == FT - 1 and s == 1))
                        if c + 1 < FT and c < len(later_groups(p, b)):
                            turn(later_groups(p, b)[c])
                    last.then_inc(s_base_used, 1)
                    n += 1
                    if prev_tile(p, b - 1) is not None:
                        turn_h(prev_tile(p, b - 1))
                    if prev_tile(p, b - 2) is not None:
                        project(prev_tile(p, b - 2))
                    if prev_tile(p, b) is not None:
                        turn_x(prev_tile(p, b))
                    for g in later_groups(p, b)[FT - 1:]:
                        turn(g)
                    if (p, b) == (0, 0):
                        pe.wait_ge(s_deg, 1)
                        tr(PS[0:1, 7, 0:P], sq_max[:, :], ident[:, :]).then_inc(s_big_t, 1)
                    if (p, b) == (0, 2):
                        pe.wait_ge(s_big, 1)
                        big = pe.value_load(big_t[0:1, 0:1], min_val=0, max_val=1)

            def gcn(j, tiles):
                r = ROWS[j]
                if tiles[0] == 0:
                    pe.wait_ge(s_counts, j + 1)
                    if j >= 6:
                        pe.wait_ge(s_relu, j - 5)
                def product(a, s, q):
                    first = a == s == q == 0
                    return mm(PS[0:r, FBANK[j], :], counts_of(j, s)[0:ROWS[a], a, 0:r], parts(a, SLOT_U, q)[0:ROWS[a], :],
                              start=first, stop=True, skip_group_check=not first)

                for a in tiles:
                    if a >= PASSES[-1][0] and j == 0:
                        pe.wait_ge(s_uev, a + 1)
                    for q in range(2):
                        if (a, q) != (NT - 1, 1):
                            product(a, 0, q)
                with pe.If(big > 0):
                    for a in tiles:
                        for q in range(2):
                            product(a, 1, q)
                if tiles[-1] == NT - 1:
                    product(NT - 1, 0, 1).then_inc(s_fin, 1)

            early_tiles, late_tiles = list(range(PASSES[-1][0])), PASSES[-1]
            begun = 0
            for i in PASSES[-1]:
                for step in (turn_x, turn_h, project):
                    step(i)
                    if begun < BEGUN and (step is not project or i == PASSES[-1][-1]):
                        if begun == 0:
                            pe.wait_ge(s_uev, early_tiles[-1] + 1)
                        gcn(begun, early_tiles)
                        begun += 1
            for j in range(NT):
                gcn(j, late_tiles if j < begun else list(range(NT)))


_INS = ['x', 'src', 'dst', 'edge_type_32', 'edge_weight1', 'L0_gnn_bases', 'L0_gnn_w_comp', 'L0_gnn_h_bias',
        'L1_gnn_W', 'L1_gnn_b']


def kernel(**inputs):
    import numpy as _np
    import concourse.bacc as _bacc
    from concourse import mybir as _mybir
    from concourse.bass_utils import run_bass_kernel_spmd as _run

    nc = _bacc.Bacc("TRN2", target_bir_lowering=False, num_devices=1)
    arrays, args = {}, []
    for name in _INS:
        a = _np.ascontiguousarray(inputs[name])
        arrays[f"in_{name}_dram"] = a
        args.append(nc.dram_tensor(f"in_{name}_dram", a.shape, _mybir.dt.from_np(a.dtype), kind="ExternalInput").ap())
    shape = inputs["x"].shape
    args.append(nc.dram_tensor("out_0_dram", shape, _mybir.dt.float32, kind="ExternalOutput").ap())
    gnn_kernel(nc, *args)
    r = _run(nc, [arrays], core_ids=[0])
    return r.results[0]["out_0_dram"]
```
